# Optimizing a Trainium2 kernel written in Bass

```python
import numpy as np
import jax
import jax.numpy as jnp

def _softmax(x, axis=-1):
    return jax.nn.softmax(x, axis=axis)

def _gelu(x):
    return jax.nn.gelu(x, approximate=True)

def _silu(x):
    return jax.nn.silu(x)

def _sigmoid(x):
    return jax.nn.sigmoid(x)

def _layernorm(x, axis=-1, eps=1e-05):
    m = jnp.mean(x, axis=axis, keepdims=True)
    v = jnp.var(x, axis=axis, keepdims=True)
    return (x - m) / jnp.sqrt(v + eps)

def _scatter_add(tgt, idx, src, axis=0):
    return tgt.at[idx].add(src)

def _segment_sum(src, seg, n):
    return jax.ops.segment_sum(src, seg, n)
kernel_name = 'mk_seq_postln_d1_jaxref_r4_6ebb38'

def setup_inputs(seed: int=0):
    np.random.seed(seed)
    _w = jnp.asarray

    def _L0_attn_setup():
        import jax, jax.numpy as jnp
        import numpy as np
        D_MODEL = 256
        N_HEAD = 16
        HEAD_D = D_MODEL // N_HEAD
        D_FF = 1024
        LN_EPS = 1e-05
        ATTN_EPS = 1e-06

        def _layer_norm(x, g, b, eps=LN_EPS):
            mu = jnp.mean(x, axis=-1, keepdims=True)
            var = jnp.var(x, axis=-1, keepdims=True)
            return (x - mu) * jax.lax.rsqrt(var + eps) * g + b

        def _linear_attention(x, qkv_w, qkv_b, out_w, out_b):
            B, N, C = x.shape
            qkv = (x @ qkv_w + qkv_b).reshape(B, N, 3, N_HEAD, HEAD_D)
            qkv = jnp.transpose(qkv, (2, 0, 3, 1, 4))
            q, k, v = (qkv[0], qkv[1], qkv[2])
            qf = jax.nn.elu(q) + 1.0
            kf = jax.nn.elu(k) + 1.0
            kv = jnp.einsum('bhnd,bhne->bhde', kf.astype(jnp.float32), v.astype(jnp.float32)).astype(v.dtype)
            y_num = jnp.einsum('bhnd,bhde->bhne', qf, kv)
            z = jnp.sum(kf.astype(jnp.float32), axis=2)
            y_den = jnp.einsum('bhnd,bhd->bhn', qf, z.astype(qf.dtype))
            y_den = jnp.maximum(y_den, ATTN_EPS)[..., None]
            y = (y_num / y_den).transpose(0, 2, 1, 3).reshape(B, N, C)
            return y @ out_w + out_b
        key = jax.random.key(seed)
        ks = jax.random.split(key, 16)
        s = 0.02
        return {'src': jax.random.normal(ks[0], (4, 1024, D_MODEL), dtype=jnp.float32), 'qkv_w': jax.random.normal(ks[1], (D_MODEL, 3 * D_MODEL), dtype=jnp.float32) * s, 'qkv_b': jax.random.normal(ks[2], (3 * D_MODEL,), dtype=jnp.float32) * s, 'out_w': jax.random.normal(ks[3], (D_MODEL, D_MODEL), dtype=jnp.float32) * s, 'out_b': jax.random.normal(ks[4], (D_MODEL,), dtype=jnp.float32) * s, 'w1': jax.random.normal(ks[5], (D_MODEL, D_FF), dtype=jnp.float32) * s, 'b1': jax.random.normal(ks[6], (D_FF,), dtype=jnp.float32) * s, 'w2': jax.random.normal(ks[7], (D_FF, D_MODEL), dtype=jnp.float32) * s, 'b2': jax.random.normal(ks[8], (D_MODEL,), dtype=jnp.float32) * s, 'g1': jnp.ones((D_MODEL,), dtype=jnp.float32), 'be1': jnp.zeros((D_MODEL,), dtype=jnp.float32), 'g2': jnp.ones((D_MODEL,), dtype=jnp.float32), 'be2': jnp.zeros((D_MODEL,), dtype=jnp.float32)}
    _L0_attn_in = _L0_attn_setup()

    def _L0_ffn_setup():
        import jax, jax.numpy as jnp
        import numpy as np
        EPS = 1e-05

        def _quantize(W):
            gamma = jnp.mean(jnp.abs(W))
            return jnp.clip(jnp.round(W / (gamma + EPS)), -1.0, 1.0)
        key = jax.random.key(seed)
        k_x, k_w1, k_b1, k_w2, k_b2 = jax.random.split(key, 5)
        n_embd = 256
        d_ff = 4 * n_embd
        B, S = (4, 1024)
        bound1 = 1.0 / np.sqrt(n_embd)
        bound2 = 1.0 / np.sqrt(d_ff)
        x = jax.random.normal(k_x, (B, S, n_embd), dtype=jnp.float32)
        W1 = jax.random.uniform(k_w1, (d_ff, n_embd), jnp.float32, -bound1, bound1)
        b1 = jax.random.uniform(k_b1, (d_ff,), jnp.float32, -bound1, bound1)
        W2 = jax.random.uniform(k_w2, (n_embd, d_ff), jnp.float32, -bound2, bound2)
        b2 = jax.random.uniform(k_b2, (n_embd,), jnp.float32, -bound2, bound2)
        return {'x': x, 'W1': W1, 'b1': b1, 'W2': W2, 'b2': b2}
    _L0_ffn_in = _L0_ffn_setup()
    _d = {'L0_attn_src': _L0_attn_in['src'], 'L0_attn_qkv_w': _L0_attn_in['qkv_w'], 'L0_attn_qkv_b': _L0_attn_in['qkv_b'], 'L0_attn_out_w': _L0_attn_in['out_w'], 'L0_attn_out_b': _L0_attn_in['out_b'], 'L0_attn_w1': _L0_attn_in['w1'], 'L0_attn_b1': _L0_attn_in['b1'], 'L0_attn_w2': _L0_attn_in['w2'], 'L0_attn_b2': _L0_attn_in['b2'], 'L0_attn_g1': _L0_attn_in['g1'], 'L0_attn_be1': _L0_attn_in['be1'], 'L0_attn_g2': _L0_attn_in['g2'], 'L0_attn_be2': _L0_attn_in['be2'], 'L0_ffn_W1': _L0_ffn_in['W1'], 'L0_ffn_b1': _L0_ffn_in['b1'], 'L0_ffn_W2': _L0_ffn_in['W2'], 'L0_ffn_b2': _L0_ffn_in['b2']}
    _x0 = _d['L0_attn_src']
    _d['L0_attn_src'] = jax.random.normal(jax.random.fold_in(jax.random.key(seed), 1), (16, 512, 256), dtype=_x0.dtype)
    del _x0
    return _d

def reference(L0_attn_src, L0_attn_qkv_w, L0_attn_qkv_b, L0_attn_out_w, L0_attn_out_b, L0_attn_w1, L0_attn_b1, L0_attn_w2, L0_attn_b2, L0_attn_g1, L0_attn_be1, L0_attn_g2, L0_attn_be2, L0_ffn_W1, L0_ffn_b1, L0_ffn_W2, L0_ffn_b2):

    def _L0_attn_ref(src, qkv_w, qkv_b, out_w, out_b, w1, b1, w2, b2, g1, be1, g2, be2):
        import jax, jax.numpy as jnp
        import numpy as np
        D_MODEL = 256
        N_HEAD = 16
        HEAD_D = D_MODEL // N_HEAD
        D_FF = 1024
        LN_EPS = 1e-05
        ATTN_EPS = 1e-06

        def _layer_norm(x, g, b, eps=LN_EPS):
            mu = jnp.mean(x, axis=-1, keepdims=True)
            var = jnp.var(x, axis=-1, keepdims=True)
            return (x - mu) * jax.lax.rsqrt(var + eps) * g + b

        def _linear_attention(x, qkv_w, qkv_b, out_w, out_b):
            B, N, C = x.shape
            qkv = (x @ qkv_w + qkv_b).reshape(B, N, 3, N_HEAD, HEAD_D)
            qkv = jnp.transpose(qkv, (2, 0, 3, 1, 4))
            q, k, v = (qkv[0], qkv[1], qkv[2])
            qf = jax.nn.elu(q) + 1.0
            kf = jax.nn.elu(k) + 1.0
            kv = jnp.einsum('bhnd,bhne->bhde', kf.astype(jnp.float32), v.astype(jnp.float32)).astype(v.dtype)
            y_num = jnp.einsum('bhnd,bhde->bhne', qf, kv)
            z = jnp.sum(kf.astype(jnp.float32), axis=2)
            y_den = jnp.einsum('bhnd,bhd->bhn', qf, z.astype(qf.dtype))
            y_den = jnp.maximum(y_den, ATTN_EPS)[..., None]
            y = (y_num / y_den).transpose(0, 2, 1, 3).reshape(B, N, C)
            return y @ out_w + out_b
        attn_out = _linear_attention(_layer_norm(src, g1, be1), qkv_w, qkv_b, out_w, out_b)
        x = src + attn_out
        h = jax.nn.gelu(_layer_norm(x, g2, be2) @ w1 + b1, approximate=False)
        return x + h @ w2 + b2

    def _L0_ffn_ref(x, W1, b1, W2, b2):
        import jax, jax.numpy as jnp
        import numpy as np
        EPS = 1e-05

        def _quantize(W):
            gamma = jnp.mean(jnp.abs(W))
            return jnp.clip(jnp.round(W / (gamma + EPS)), -1.0, 1.0)
        Wq1 = _quantize(W1)
        Wq2 = _quantize(W2)
        h = jax.nn.relu(jnp.einsum('bsd,fd->bsf', x, Wq1) + b1)
        out = jnp.einsum('bsf,df->bsd', h, Wq2) + b2
        return out
    x = L0_attn_src
    x = _layernorm(x + _L0_attn_ref(x, L0_attn_qkv_w, L0_attn_qkv_b, L0_attn_out_w, L0_attn_out_b, L0_attn_w1, L0_attn_b1, L0_attn_w2, L0_attn_b2, L0_attn_g1, L0_attn_be1, L0_attn_g2, L0_attn_be2), axis=-1)
    x = _layernorm(x + _L0_ffn_ref(x, L0_ffn_W1, L0_ffn_b1, L0_ffn_W2, L0_ffn_b2), axis=-1)
    return x

_drawn_inputs = setup_inputs


def setup_inputs(seed=0):
    import zlib

    import numpy as np

    out = dict(_drawn_inputs(seed))
    spreads = {'L0_attn_g1': (1.0, 0.6),
     'L0_attn_be1': (0.0, 0.8),
     'L0_attn_g2': (1.0, 0.6),
     'L0_attn_be2': (0.0, 2.0)}
    factors = {'L0_attn_qkv_w': 8.0,
     'L0_attn_qkv_b': 8.0,
     'L0_attn_out_w': 8.0,
     'L0_attn_out_b': 17.436,
     'L0_attn_b1': 38.609,
     'L0_attn_b2': 16.693,
     'L0_ffn_b1': 8.0,
     'L0_ffn_b2': 64.0}
    for name, (base, spread) in spreads.items():
        noise = np.random.default_rng([zlib.crc32(name.encode()), seed]).standard_normal(out[name].shape)
        drawn = base * np.exp(spread * noise) if base else spread * noise
        out[name] = jnp.asarray(drawn.astype(out[name].dtype))
    for name, factor in factors.items():
        out[name] = (out[name] * factor).astype(out[name].dtype)
    return out
```

```python
from contextlib import ExitStack

import concourse.bass as bass
from concourse import mybir

P = 128
D = 256
F = 1024
S = 16
N = 512
T = N // P
C = D // P
M = F // P
HEADS = 16
HD = D // HEADS
HC = P // HD
VW = P + 2
KW = P + HC
LN_EPS = 1e-5
ATTN_EPS = 1e-6
Q_EPS = 1e-5

F32 = mybir.dt.float32
F32R = mybir.dt.float32r
ALU = mybir.AluOpType
ACT = mybir.ActivationFunctionType
AX = mybir.AxisListType

COL_G1, COL_BE1, COL_G2, COL_BE2, COL_BQ, COL_B1, COL_FB1, COLS = 0, 2, 4, 6, 8, 10, 18, 26
ROW_KV, ROW_OUT, ROW_B2, ROW_FB2, ROWS = 0, 512, 768, 1024, 1280


def exists(i, back):
    return not isinstance(i, int) or i >= back


def build(nc, src, qkv_w, out_w, w1, w2, fw1, fw2, cols_in, rows_in, const_in, out):
    src_rows = src.rearrange("s (p t) d -> (s p) (t d)", t=T)
    out_rows = out.rearrange("s (p t) d -> (s p) (t d)", t=T)
    x_dram = nc.dram_tensor("x_dram", (S * P, T * D), F32, kind="Internal").ap()

    with ExitStack() as both:
        def sb(stack, name, shape, dt=F32):
            return stack.enter_context(nc.sbuf_tensor(name, shape, dt))

        def sem(stack, *names):
            return [stack.enter_context(nc.semaphore(n)) for n in names]

        wqkv = [sb(both, f"wqkv_{k}", [P, C, 3 * D], F32R) for k in "hl"]
        wout = [sb(both, f"wout_{k}", [P, C, D], F32R) for k in "hl"]
        w1s = [sb(both, f"w1_{k}", [P, C, F], F32R) for k in "hl"]
        w2s = [sb(both, f"w2_{k}", [P, M, D], F32R) for k in "hl"]
        fq1 = sb(both, "fq1", [P, C, F], F32R)
        fq2 = sb(both, "fq2", [P, M, D], F32R)
        cols = sb(both, "cols", [P, COLS])
        ident = sb(both, "ident", [P, P])
        b1c = sb(both, "b1c", [P, M])
        row_b2 = sb(both, "row_b2", [P, D])
        row_fb2 = sb(both, "row_fb2", [P, D])
        half4 = sb(both, "half4", [P, T])
        minus1 = sb(both, "minus1", [P, 1])

        def moments_level(level, dve, bn, stats, levels, moments, scaled_to, ready, pool_read, j):
            pair, dif, var = moments
            veps, nmean = scaled_to
            if level == 0:
                dve.wait_ge(stats, T * j + T)
                nc.vector.tensor_tensor(pair[:], bn[:, :, 1:3], bn[:, :, 4:6], ALU.add).then_inc(levels, 1)
                nc.vector.tensor_tensor(dif[:], bn[:, :, 1], bn[:, :, 4], ALU.subtract).then_inc(levels, 1)
            if level == 1:
                if exists(j, 1):
                    dve.wait_ge(pool_read, 2 * j)
                dve.wait_ge(levels, 4 * j + 1)
                nc.vector.tensor_scalar(nmean[:], pair[:, :, 0], -0.5, None, ALU.mult).then_inc(ready, 1)
                dve.wait_ge(levels, 4 * j + 2)
                nc.vector.scalar_tensor_tensor(out=dif[:], in0=dif[:], scalar=0.25, in1=dif[:], op0=ALU.mult,
                                               op1=ALU.mult).then_inc(levels, 1)
            if level == 2:
                dve.wait_ge(levels, 4 * j + 3)
                nc.vector.scalar_tensor_tensor(out=var[:], in0=pair[:, :, 1], scalar=1.0 / D, in1=dif[:],
                                               op0=ALU.mult, op1=ALU.add).then_inc(levels, 1)
            if level == 3:
                dve.wait_ge(levels, 4 * j + 4)
                nc.vector.tensor_scalar(veps[:], var[:], LN_EPS, None, ALU.add).then_inc(ready, 1)

        def finish_scale(pool, veps, nmean, rstd, nmr, ready, steps, used, j):
            if exists(j, 1):
                pool.wait_ge(used, T * j)
            pool.wait_ge(ready, 2 * j + 2)
            nc.gpsimd.tensor_tensor(rstd[:], veps[:], half4[:], ALU.pow).then_inc(steps, 1)
            pool.wait_ge(steps, 2 * j + 1)
            nc.gpsimd.tensor_tensor(nmr[:], nmean[:], rstd[:], ALU.mult).then_inc(steps, 1)

        passes3 = [(0, 0), (0, 1), (1, 0)]

        with ExitStack() as ph:
            qkv_raw = sb(ph, "qkv_raw", [P, C, 3 * D])
            out_raw = sb(ph, "out_raw", [P, C, D])
            w1_raw = sb(ph, "w1_raw", [P, C, F])
            w2_raw = sb(ph, "w2_raw", [P, M, D])
            f1_raw = sb(ph, "f1_raw", [P, C, F])
            f2_raw = sb(ph, "f2_raw", [P, M, D])
            rows = sb(ph, "rows", [1, ROWS])
            mask = sb(ph, "mask", [P, KW])
            ones = sb(ph, "ones", [P, P])
            be1_wide = sb(ph, "be1_wide", [P, C, P])
            row_k1 = sb(ph, "row_k1", [P, D])
            row_out = sb(ph, "row_out", [P, D])
            bv_mask = sb(ph, "bv_mask", [P, C, P])
            bq_neg = sb(ph, "bq_neg", [P, C])
            bq_one = sb(ph, "bq_one", [P, C])
            abs_out = sb(ph, "abs_out", [P, D])
            abs_sum = sb(ph, "abs_sum", [P, 2, 8])
            abs_tot = sb(ph, "abs_tot", [P, 2])
            thr = sb(ph, "thr", [P, 2])
            thr_neg = sb(ph, "thr_neg", [P, 2])
            below = sb(ph, "below", [P, 2, 2 * F])

            src_sb = sb(ph, "src_sb", [P, 2, T, D])
            srcb = sb(ph, "srcb", [P, 2, T, D])
            bn = sb(ph, "bn", [P, T, 6])
            moments = (sb(ph, "pair", [P, T, 2]), sb(ph, "dif", [P, T]), sb(ph, "var", [P, T]))
            veps = sb(ph, "veps", [P, T])
            nmean = sb(ph, "nmean", [P, T])
            rstd = sb(ph, "rstd", [P, T])
            nmr = sb(ph, "nmr", [P, T])
            xhat = sb(ph, "xhat", [P, T, D])
            xT = [sb(ph, f"xT_{k}", [P, C, N], F32R) for k in "hl"]
            k1 = sb(ph, "k1", [P, T, D])
            ek = sb(ph, "ek", [P, T, D])
            kf = sb(ph, "kf", [P, T, D])
            v_sb = sb(ph, "v_sb", [P, T, C, VW])
            eq = sb(ph, "eq", [P, C, N])
            qf = sb(ph, "qf", [P, C, N])
            kvm = sb(ph, "kvm", [P, C, P])
            kvz = sb(ph, "kvz", [P, C, KW])
            den = sb(ph, "den", [P, 2, 2 * C, HC])
            rden = sb(ph, "rden", [P, 2, 2 * C, HC])
            y_sb = sb(ph, "y_sb", [P, T, D])
            yT = [sb(ph, f"yT_{k}", [P, C, N], F32R) for k in "hl"]
            x_sb = sb(ph, "x_sb", [P, T, D])

            pT = ph.enter_context(nc.psum_tensor("pT", [P, C, N], F32))
            pKV = ph.enter_context(nc.psum_tensor("pKV", [P, 2, N], F32))
            pQ = ph.enter_context(nc.psum_tensor("pQ", [P, 2, N], F32))
            pS = ph.enter_context(nc.psum_tensor("pS", [P, N], F32))
            pO = ph.enter_context(nc.psum_tensor("pO", [P, N], F32))

            (s_vec, s_wqkv, s_wout, s_wmlp, s_wffn, s_const, s_src0, s_src1, s_stored,
             setup_dve, abs_done, setup_act, setup_pe_mm, thr_pe, scaled, wsplit, brow_done, bq_done, thr_done, tern_done) = sem(
                ph, "s_vec", "s_wqkv", "s_wout", "s_wmlp", "s_wffn", "s_const", "s_src0", "s_src1",
                "s_stored", "setup_dve", "abs_done", "setup_act", "setup_pe_mm", "thr_pe", "scaled", "wsplit", "brow_done",
                "bq_done", "thr_done", "tern_done")
            s_src = [s_src0, s_src1]
            (stats_done, levels, moments_done, scale_done, xhat_done, srcb_done, xTp, xh_done, xl_done, kv_mm, k1_done,
             v_done, ek_done, kf_done, q_mm, rq_done, eq_done, qf_done, s_mm, kvm_done, kvz_done,
             num_mm, den_done, rden_done, y_done, yTp, yh_done, yl_done, o_mm, x_done) = sem(
                ph, "stats_done", "levels", "moments_done", "scale_done", "xhat_done", "srcb_done", "xTp", "xh_done", "xl_done",
                "kv_mm", "k1_done", "v_done", "ek_done", "kf_done", "q_mm", "rq_done", "eq_done",
                "qf_done", "s_mm", "kvm_done", "kvz_done", "num_mm", "den_done", "rden_done",
                "y_done", "yTp", "yh_done", "yl_done", "o_mm", "x_done")

            block = ph.enter_context(nc.Block())

            def src_landed(engine, j, slot):
                engine.wait_ge(s_src[slot], 16 * (j // 2 + 1) if isinstance(j, int) else j * 8 + (8 if slot else 16))

            @block.sync
            def _(sp):
                sp.dma_start(src_sb[:, 0], src_rows[0:P, :]).then_inc(s_src[0], 16)
                sp.dma_start(qkv_raw[:], qkv_w.rearrange("(c p) n -> p c n", p=P)).then_inc(s_wqkv, 16)
                sp.dma_start(src_sb[:, 1], src_rows[P:2 * P, :]).then_inc(s_src[1], 16)
                sp.dma_start(out_raw[:], out_w.rearrange("(c p) n -> p c n", p=P)).then_inc(s_wout, 16)
                sp.dma_start(w1_raw[:], w1.rearrange("(c p) n -> p c n", p=P)).then_inc(s_wmlp, 16)
                sp.dma_start(w2_raw[:], w2.rearrange("(m p) n -> p m n", p=P)).then_inc(s_wmlp, 16)
                sp.dma_start(f1_raw[:], fw1.rearrange("(c p) n -> p c n", p=P)).then_inc(s_wffn, 16)
                sp.dma_start(f2_raw[:], fw2.rearrange("(m p) n -> p m n", p=P)).then_inc(s_wffn, 16)

                def step(i, slot, more):
                    if more:
                        sp.wait_ge(srcb_done, i + 1)
                        sp.wait_ge(xhat_done, T * i + T)
                        sp.dma_start(src_sb[:, slot], src_rows[bass.ds((i + 2) * P, P), :]
                                     if not isinstance(i, int) else src_rows[(i + 2) * P:(i + 3) * P, :]
                                     ).then_inc(s_src[slot], 16)
                    if exists(i, 1):
                        sp.wait_ge(x_done, 2 * i)
                        sp.dma_start(x_dram[bass.ds((i - 1) * P, P), :]
                                     if not isinstance(i, int) else x_dram[(i - 1) * P:i * P, :],
                                     x_sb[:]).then_inc(s_stored, 16)

                step(0, 0, True)
                with sp.Fori(1, S - 3, 2) as i:
                    step(i, 1, True)
                    step(i + 1, 0, True)
                step(S - 3, 1, True)
                step(S - 2, 0, False)
                step(S - 1, 1, False)
                step(S, 0, False)
                sp.wait_ge(s_stored, 16 * S)

            @block.gpsimd
            def _(pool):
                pool.memset(half4[:], -0.5).then_inc(setup_act, 1)
                pool.memset(minus1[:], -1.0).then_inc(setup_act, 1)
                pool.memset(v_sb[:, :, :, P:VW], 1.0).then_inc(setup_act, 1)
                pool.wait_ge(setup_act, 3)

                def add_bias(j, slot):
                    if exists(j, 2):
                        pool.wait_ge(x_done, 2 * j - 2)
                    src_landed(pool, j, slot)
                    if isinstance(j, int) and j == 0:
                        pool.wait_ge(brow_done, 3)
                    for t in range(T):
                        last = nc.gpsimd.tensor_tensor(srcb[:, slot, t], src_sb[:, slot, t], row_out[:], ALU.add)
                    last.then_inc(srcb_done, 1)

                def scale(j):
                    finish_scale(pool, veps, nmean, rstd, nmr, moments_done, scale_done, xhat_done, j)

                scale(0)
                scale(1)
                add_bias(0, 0)

                def step(i, slot, more):
                    if more:
                        scale(i + 2)
                    add_bias(i + 1, 1 - slot)

                step(0, 0, True)
                with pool.Fori(1, S - 3, 2) as i:
                    step(i, 1, True)
                    step(i + 1, 0, True)
                step(S - 3, 1, True)
                step(S - 2, 0, False)

            @block.scalar
            def _(act):
                act.dma_start(cols[:], cols_in).then_inc(s_vec, 16)
                act.dma_start(rows[:], rows_in).then_inc(s_vec, 16)
                act.dma_start(ident[:], const_in[:, 0:P]).then_inc(s_const, 16)
                act.dma_start(mask[:], const_in[:, P:P + KW]).then_inc(s_const, 16)

                def split_xT(j):
                    for c in range(C):
                        act.wait_ge(xTp, 2 * j + c + 1)
                        nc.scalar.activation(xT[0][:, c], pT[:, c], ACT.Copy).then_inc(xh_done, 1)

                def normalise(j, slot, tiles):
                    if exists(j, 1):
                        act.wait_ge(xTp, 2 * j)
                    act.wait_ge(scale_done, 2 * j + 2)
                    for t in tiles:
                        nc.scalar.activation(xhat[:, t], src_sb[:, slot, t], ACT.Identity, bias=nmr[:, t:t + 1],
                                             scale=rstd[:, t:t + 1]).then_inc(xhat_done, 1)

                src_landed(act, 0, 0)
                normalise(0, 0, range(T))
                split_xT(0)

                def v_tile(i, t):
                    act.wait_ge(k1_done, T * i + t + 1)
                    nc.scalar.activation(v_sb[:, t, :, 0:P],
                                         pKV[:, 1 - t % 2, D:2 * D].rearrange("p (c n) -> p c n", c=C),
                                         ACT.Copy).then_inc(v_done, 1)

                def k_exp(i, h):
                    nc.scalar.activation(ek[:, 2 * h:2 * h + 2], k1[:, 2 * h:2 * h + 2], ACT.Exp,
                                         bias=minus1[:]).then_inc(ek_done, 1)

                def step(i, slot, front, ahead):
                    if front:
                        if ahead:
                            src_landed(act, i + 1, 1 - slot)
                            normalise(i + 1, 1 - slot, range(T))
                        if exists(i, 1):
                            act.wait_ge(s_mm, i)
                        v_tile(i, 0)
                        v_tile(i, 1)
                        k_exp(i, 0)
                        v_tile(i, 2)
                        v_tile(i, 3)
                        k_exp(i, 1)
                    if exists(i, 1):
                        split_y(i)
                    if front:
                        for m in range(C):
                            if exists(i, 1):
                                act.wait_ge(qf_done, 2 * i)
                            act.wait_ge(q_mm, 2 * i + m + 1)
                            nc.scalar.activation(eq[:, m], pQ[:, m], ACT.Relu, bias=bq_neg[:, m:m + 1],
                                                 scale=-1.0).then_inc(rq_done, 1)
                            act.wait_ge(rq_done, 2 * i + m + 1)
                            nc.scalar.activation(eq[:, m], eq[:, m], ACT.Exp, scale=-1.0).then_inc(eq_done, 1)
                        if ahead:
                            split_xT(i + 1)

                def split_y(i):
                    for c in range(C):
                        act.wait_ge(yTp, 2 * (i - 1) + c + 1)
                        nc.scalar.activation(yT[0][:, c], pT[:, c], ACT.Copy).then_inc(yh_done, 1)

                act.wait_ge(setup_act, 3)
                act.wait_ge(bq_done, 2 * C)
                step(0, 0, True, True)
                act.wait_ge(s_wffn, 32)
                for n, raw in enumerate((f1_raw, f2_raw)):
                    flat = raw[:].rearrange("p a b -> p (a b)")
                    for k in range(8):
                        if n or k:
                            act.wait_ge(abs_done, 8 * n + k)
                        nc.scalar.activation(abs_out[:], flat[:, k * D:(k + 1) * D], ACT.Abs,
                                             accum_out=abs_sum[:, n, k:k + 1]).then_inc(abs_done, 1)
                with act.Fori(1, S - 1, 2) as i:
                    step(i, 1, True, True)
                    step(i + 1, 0, True, True)
                step(S - 1, 1, True, False)
                step(S, 0, False, False)

            @block.vector
            def _(dve):
                def stats(j, slot):
                    src_landed(dve, j, slot)
                    for t in range(T):
                        nc.vector.bn_stats(bn[:, t], src_sb[:, slot, t]).then_inc(stats_done, 1)

                def moment(level, j):
                    moments_level(level, dve, bn, stats_done, levels, moments, (veps, nmean), moments_done,
                                  scale_done, j)

                def split_xT(j):
                    for c in range(C):
                        dve.wait_ge(xh_done, 2 * j + c + 1)
                        nc.vector.tensor_tensor(xT[1][:, c], pT[:, c], xT[0][:, c].bitcast(F32),
                                                ALU.subtract).then_inc(xl_done, 1)

                def split_y(i):
                    for c in range(C):
                        dve.wait_ge(yh_done, 2 * (i - 1) + c + 1)
                        nc.vector.tensor_tensor(yT[1][:, c], pT[:, c], yT[0][:, c].bitcast(F32),
                                                ALU.subtract).then_inc(yl_done, 1)

                def residual(i, slot):
                    for h in range(2):
                        dve.wait_ge(o_mm, 2 * (i - 1) + h + 1)
                        if h == 0:
                            dve.wait_ge(srcb_done, i)
                            if exists(i, 2):
                                dve.wait_ge(s_stored, 16 * (i - 1))
                        p = pO[:, :] if h == 0 else pKV[:, 0]
                        nc.vector.tensor_tensor(x_sb[:, 2 * h:2 * h + 2], p.rearrange("p (t d) -> p t d", t=2),
                                                srcb[:, 1 - slot, 2 * h:2 * h + 2], ALU.add).then_inc(x_done, 1)

                dve.memset(ones[:], 1.0).then_inc(setup_dve, 1)
                for j in range(2):
                    stats(j, j)
                    for level in range(4):
                        moment(level, j)
                dve.wait_ge(s_vec, 32)
                dve.wait_ge(s_wqkv, 16)
                dve.wait_ge(setup_dve, 1)
                for c in range(C):
                    nc.vector.tensor_scalar(be1_wide[:, c], ones[:], cols[:, COL_BE1 + c:COL_BE1 + c + 1], None,
                                            ALU.mult).then_inc(setup_dve, 1)
                for c in range(C):
                    nc.vector.tensor_scalar(below[:, 0, c * 3 * D:(c + 1) * 3 * D], qkv_raw[:, c],
                                            cols[:, COL_G1 + c:COL_G1 + c + 1], None, ALU.mult).then_inc(scaled, 1)
                qkv_g = below[:, 0, 0:C * 3 * D].rearrange("p (c n) -> p c n", c=C)
                dve.wait_ge(scaled, C)
                for c in range(C):
                    nc.vector.tensor_copy(wqkv[0][:, c], qkv_g[:, c]).then_inc(wsplit, 1)
                for c in range(C):
                    dve.wait_ge(wsplit, c + 1)
                    nc.vector.tensor_tensor(wqkv[1][:, c], qkv_g[:, c], wqkv[0][:, c].bitcast(F32),
                                            ALU.subtract).then_inc(wsplit, 1)
                dve.wait_ge(setup_pe_mm, 1)
                for m in range(C):
                    b = cols[:, COL_BQ + m:COL_BQ + m + 1]
                    nc.vector.tensor_scalar(bq_neg[:, m:m + 1], pS[:, m:m + 1], b, -1.0, ALU.add,
                                            ALU.mult).then_inc(bq_done, 1)
                    nc.vector.tensor_scalar(bq_one[:, m:m + 1], pS[:, m:m + 1], b, 1.0, ALU.add,
                                            ALU.add).then_inc(bq_done, 1)
                nc.vector.tensor_scalar(row_k1[:], pQ[:, 0, 0:D], 1.0, None, ALU.add).then_inc(brow_done, 1)
                dve.wait_ge(s_const, 32)
                nc.vector.tensor_tensor(bv_mask[:], pQ[:, 0, D:2 * D].rearrange("p (c n) -> p c n", c=C),
                                        mask[:, 0:P].rearrange("p (o n) -> p o n", o=1).broadcast_to([P, C, P]),
                                        ALU.mult).then_inc(brow_done, 1)
                nc.vector.tensor_copy(row_out[:], pQ[:, 1, 0:D]).then_inc(brow_done, 1)
                nc.vector.tensor_copy(row_b2[:], pQ[:, 1, D:2 * D]).then_inc(brow_done, 1)
                nc.vector.tensor_copy(row_fb2[:], pO[:, 0:D]).then_inc(brow_done, 1)
                split_xT(0)
                dve.wait_ge(s_wout, 16)
                nc.vector.tensor_copy(wout[0][:], out_raw[:]).then_inc(wsplit, 1)
                dve.wait_ge(wsplit, 2 * C + 1)
                nc.vector.tensor_tensor(wout[1][:], out_raw[:], wout[0][:].bitcast(F32),
                                        ALU.subtract).then_inc(wsplit, 1)

                def k_tile(i, t):
                    dve.wait_ge(kv_mm, T * i + t + 1)
                    nc.vector.tensor_tensor(k1[:, t], pKV[:, 1 - t % 2, 0:D], row_k1[:], ALU.add).then_inc(k1_done, 1)

                def k_features(i, h):
                    dve.wait_ge(ek_done, 2 * i + h + 1)
                    nc.vector.scalar_tensor_tensor(
                        out=kf[:, 2 * h:2 * h + 2], in0=ek[:, 2 * h:2 * h + 2], scalar=1.0,
                        in1=k1[:, 2 * h:2 * h + 2], op0=ALU.min, op1=ALU.max).then_inc(kf_done, 1)

                def q_features(i, m):
                    dve.wait_ge(eq_done, 2 * i + m + 1)
                    nc.vector.scalar_tensor_tensor(
                        out=qf[:, m], in0=pQ[:, m], scalar=bq_one[:, m:m + 1], in1=eq[:, m],
                        op0=ALU.add, op1=ALU.max).then_inc(qf_done, 1)

                def kv_state(i):
                    st = pS[:, 0:C * VW].rearrange("p (c n) -> p c n", c=C)
                    dve.wait_ge(s_mm, i + 1)
                    nc.vector.tensor_tensor(kvm[:], st[:, :, 0:P],
                                            mask[:, 0:P].rearrange("p (o n) -> p o n", o=1).broadcast_to([P, C, P]),
                                            ALU.mult).then_inc(kvm_done, 1)
                    for c in range(C):
                        nc.vector.tensor_scalar(kvz[:, c, P:KW], mask[:, P:KW], st[:, c, P:P + 1], None,
                                                ALU.mult).then_inc(kvz_done, 1)
                    dve.wait_ge(kvm_done, i + 1)
                    for c in range(C):
                        nc.vector.scalar_tensor_tensor(
                            out=kvz[:, c, 0:P], in0=bv_mask[:, c], scalar=st[:, c, P:P + 1], in1=kvm[:, c],
                            op0=ALU.mult, op1=ALU.add).then_inc(kvz_done, 1)

                def divide(i, h):
                    num = (pQ if h == 0 else pT)[:].rearrange("p t (c n) -> p (t c) n", c=C)
                    dve.wait_ge(num_mm, 2 * i + h + 1)
                    nc.vector.tensor_scalar(den[:, h], num[:, :, P:KW], ATTN_EPS, None, ALU.max).then_inc(den_done, 1)
                    dve.wait_ge(den_done, 2 * i + h + 1)
                    nc.vector.reciprocal(rden[:, h], den[:, h]).then_inc(rden_done, 1)
                    dve.wait_ge(rden_done, 2 * i + h + 1)
                    nc.vector.tensor_tensor(
                        y_sb[:, 2 * h:2 * h + 2].rearrange("p t (c h e) -> p (t c) h e", c=C, h=HC),
                        num[:, :, 0:P].rearrange("p a (h e) -> p a h e", h=HC),
                        rden[:, h].rearrange("p a (h o) -> p a h o", o=1).broadcast_to([P, 2 * C, HC, HD]),
                        ALU.mult).then_inc(y_done, 1)

                def step(i, slot, front, ahead):
                    if front:
                        k_tile(i, 0)
                        k_tile(i, 1)
                        k_tile(i, 2)
                        k_features(i, 0)
                        k_tile(i, 3)
                        k_features(i, 1)
                    if exists(i, 1):
                        split_y(i)
                    if front:
                        if ahead == 2:
                            stats(i + 2, slot)
                            moment(0, i + 2)
                        q_features(i, 0)
                        if ahead == 2:
                            moment(1, i + 2)
                        q_features(i, 1)
                        if ahead == 2:
                            moment(2, i + 2)
                        kv_state(i)
                        if ahead == 2:
                            moment(3, i + 2)
                        if ahead:
                            split_xT(i + 1)
                    if exists(i, 1):
                        residual(i, slot)
                    if front:
                        divide(i, 0)
                        divide(i, 1)

                dve.wait_ge(brow_done, 5)
                step(0, 0, True, 2)

                dve.wait_ge(s_wmlp, 32)
                w1_g = below[:, 0, :].rearrange("p (c n) -> p c n", c=C)
                for c in range(C):
                    nc.vector.tensor_scalar(w1_g[:, c], w1_raw[:, c], cols[:, COL_G2 + c:COL_G2 + c + 1], None,
                                            ALU.mult).then_inc(scaled, 1)
                nc.vector.tensor_copy(w2s[0][:], w2_raw[:]).then_inc(wsplit, 1)
                dve.wait_ge(scaled, 2 * C)
                nc.vector.tensor_copy(w1s[0][:], w1_g).then_inc(wsplit, 1)
                dve.wait_ge(wsplit, 2 * C + 3)
                nc.vector.tensor_tensor(w2s[1][:], w2_raw[:], w2s[0][:].bitcast(F32), ALU.subtract).then_inc(wsplit, 1)
                dve.wait_ge(wsplit, 2 * C + 4)
                nc.vector.tensor_tensor(w1s[1][:], w1_g, w1s[0][:].bitcast(F32), ALU.subtract).then_inc(wsplit, 1)
                dve.wait_ge(abs_done, 16)
                nc.vector.tensor_reduce(abs_tot[:], abs_sum[:], AX.X, ALU.add).then_inc(thr_done, 1)
                dve.wait_ge(thr_pe, 1)
                nc.vector.tensor_scalar(thr[:], pS[:, 0:2], 1.0 / (D * F), Q_EPS, ALU.mult, ALU.add).then_inc(thr_done, 1)
                dve.wait_ge(thr_done, 2)
                nc.vector.tensor_scalar(thr_neg[:], thr[:], -0.5, None, ALU.mult).then_inc(thr_done, 1)
                dve.wait_ge(thr_done, 3)
                nc.vector.tensor_scalar(thr[:], thr[:], 0.5, None, ALU.mult).then_inc(thr_done, 1)
                nc.vector.tensor_tensor(b1c[:], pS[:, 8:8 + M], cols[:, COL_B1:COL_B1 + M], ALU.add).then_inc(thr_done, 1)
                dve.wait_ge(thr_done, 5)
                dve.wait_ge(wsplit, 2 * C + 6)
                for n, raw in enumerate((f1_raw, f2_raw)):
                    nc.vector.tensor_scalar(below[:, n], raw[:].rearrange("p a b -> p (a b)"),
                                            thr_neg[:, n:n + 1], None, ALU.is_lt).then_inc(tern_done, 1)
                for n, (raw, q) in enumerate(((f1_raw, fq1), (f2_raw, fq2))):
                    dve.wait_ge(tern_done, n + 1)
                    nc.vector.scalar_tensor_tensor(
                        out=q[:].rearrange("p a b -> p (a b)"), in0=raw[:].rearrange("p a b -> p (a b)"),
                        scalar=thr[:, n:n + 1], in1=below[:, n], op0=ALU.is_gt, op1=ALU.subtract).then_inc(tern_done, 1)

                with dve.Fori(1, S - 3, 2) as i:
                    step(i, 1, True, 2)
                    step(i + 1, 0, True, 2)
                step(S - 3, 1, True, 2)
                step(S - 2, 0, True, 1)
                step(S - 1, 1, True, 0)
                step(S, 0, False, 0)

            @block.tensor
            def _(pe):
                pe.wait_ge(s_wqkv, 16)
                pe.wait_ge(s_vec, 32)
                pe.wait_ge(s_const, 32)
                pe.wait_ge(setup_dve, 1 + C)
                for m in range(C):
                    for c in range(C):
                        nc.tensor.matmul(pS[:, m:m + 1], qkv_raw[:, c, m * P:(m + 1) * P],
                                         cols[:, COL_BE1 + c:COL_BE1 + c + 1], start=c == 0, stop=c == C - 1)
                for c in range(C):
                    nc.tensor.matmul(pQ[:, 0], be1_wide[:, c], qkv_raw[:, c, D:3 * D], start=c == 0, stop=False)
                nc.tensor.matmul(pQ[:, 0], ones[0:1], rows[:, ROW_KV:ROW_KV + 2 * D], start=False, stop=True)
                nc.tensor.matmul(pQ[:, 1], ones[0:1], rows[:, ROW_OUT:ROW_OUT + 2 * D], start=True, stop=True)
                nc.tensor.matmul(pO[:, 0:D], ones[0:1], rows[:, ROW_FB2:ROW_FB2 + D], start=True,
                                 stop=True).then_inc(setup_pe_mm, 1)

                def transposes(src_tile, ready):
                    for c in range(C):
                        for t in range(T):
                            mm = nc.tensor.transpose(pT[:, c, t * P:(t + 1) * P], src_tile[:, t, c * P:(c + 1) * P],
                                                     ident[:])
                        mm.then_inc(ready, 1)

                pe.wait_ge(xhat_done, T)
                transposes(xhat, xTp)

                def step(i, front, ahead):
                    if front:
                        pe.wait_ge(xh_done, 2 * i + 2)
                        pe.wait_ge(xl_done, 2 * i + 2)
                        for t in range(T):
                            if t == 1 and exists(i, 2):
                                pe.wait_ge(x_done, 2 * (i - 1))
                            if t >= 2:
                                pe.wait_ge(k1_done, T * i + t - 1)
                                pe.wait_ge(v_done, T * i + t - 1)
                            for n, (a, w) in enumerate(passes3):
                                for c in range(C):
                                    mm = nc.tensor.matmul(pKV[:, 1 - t % 2], xT[a][:, c, t * P:(t + 1) * P],
                                                          wqkv[w][:, c, D:3 * D], start=n == 0 and c == 0,
                                                          stop=n == 2 and c == C - 1)
                            mm.then_inc(kv_mm, 1)
                    if exists(i, 1):
                        pe.wait_ge(y_done, 2 * i)
                        transposes(y_sb, yTp)
                    if front:
                        for m in range(C):
                            for n, (a, w) in enumerate(passes3):
                                for c in range(C):
                                    mm = nc.tensor.matmul(pQ[:, m], wqkv[w][:, c, m * P:(m + 1) * P], xT[a][:, c],
                                                          start=n == 0 and c == 0, stop=n == 2 and c == C - 1)
                            mm.then_inc(q_mm, 1)
                        pe.wait_ge(kf_done, 2 * i + 2)
                        pe.wait_ge(v_done, T * i + T)
                        for c in range(C):
                            for t in range(T):
                                mm = nc.tensor.matmul(pS[:, c * VW:(c + 1) * VW], kf[:, t, c * P:(c + 1) * P],
                                                      v_sb[:, t, c], start=t == 0, stop=t == T - 1)
                        mm.then_inc(s_mm, 1)
                    if exists(i, 1):
                        pe.wait_ge(yh_done, 2 * i)
                        pe.wait_ge(yl_done, 2 * i)
                    if ahead:
                        pe.wait_ge(xhat_done, T * (i + 1) + T)
                        transposes(xhat, xTp)
                    if exists(i, 1):
                        for t in range(T):
                            o = pO[:, t % 2 * D:(t % 2 + 1) * D] if t < 2 else pKV[:, 0, t % 2 * D:(t % 2 + 1) * D]
                            if t == 0 and not front:
                                pe.wait_ge(x_done, 2 * (i - 1))
                            for n, (a, w) in enumerate(passes3):
                                for c in range(C):
                                    mm = nc.tensor.matmul(o, yT[a][:, c, t * P:(t + 1) * P], wout[w][:, c],
                                                          start=n == 0 and c == 0, stop=n == 2 and c == C - 1)
                            if t % 2:
                                mm.then_inc(o_mm, 1)
                    if front:
                        pe.wait_ge(kvz_done, 2 * C * (i + 1))
                        pe.wait_ge(qf_done, 2 * i + 2)
                        for t in range(T):
                            if t == 2 and ahead:
                                pe.wait_ge(xl_done, 2 * (i + 2))
                            for c in range(C):
                                mm = nc.tensor.matmul((pQ if t < 2 else pT)[:, t % 2, c * D:c * D + KW],
                                                      qf[:, c, t * P:(t + 1) * P], kvz[:, c], start=True, stop=True)
                            if t % 2:
                                mm.then_inc(num_mm, 1)

                pe.wait_ge(wsplit, 2 * C)
                pe.wait_ge(brow_done, 5)
                step(0, True, True)
                pe.wait_ge(kvz_done, 2 * C)
                pe.wait_ge(thr_done, 1)
                nc.tensor.matmul(pS[:, 0:2], ones[:], abs_tot[:], start=True, stop=True)
                pe.wait_ge(s_wmlp, 32)
                for m in range(M):
                    for c in range(C):
                        mm = nc.tensor.matmul(pS[:, 8 + m:9 + m], w1_raw[:, c, m * P:(m + 1) * P],
                                              cols[:, COL_BE2 + c:COL_BE2 + c + 1], start=c == 0, stop=c == C - 1)
                mm.then_inc(thr_pe, 1)
                pe.wait_ge(wsplit, 2 * C + 2)
                pe.wait_ge(thr_done, 5)
                with pe.Fori(1, S - 1) as i:
                    step(i, True, True)
                step(S - 1, True, False)
                step(S, False, False)

        with ExitStack() as ph:
            x_in = sb(ph, "x_in", [P, T, D])
            r_sb = sb(ph, "r_sb", [P, T, D])
            x1 = sb(ph, "x1", [P, T, D])
            x1T = [sb(ph, f"x1T_{k}", [P, C, N], F32R) for k in "hl"]
            g_sb = sb(ph, "g_sb", [P, 3, N])
            hT = [sb(ph, f"hT_{k}", [P, M, N], F32R) for k in "hl"]
            r2 = sb(ph, "r2", [P, T, D])
            x2 = sb(ph, "x2", [P, T, D])
            x2b = sb(ph, "x2b", [P, T, D])
            x2T = [sb(ph, f"x2T_{k}", [P, C, N], F32R) for k in "hl"]
            RELU_SLOTS = 6
            u_sb = sb(ph, "u_sb", [P, RELU_SLOTS, N])
            uT = [sb(ph, f"uT_{k}", [P, M, N], F32R) for k in "hl"]
            z_sb = sb(ph, "z_sb", [P, T, D])
            o_sb = sb(ph, "o_sb", [P, T, D])
            bn = [sb(ph, f"bn{n}", [P, T, 6]) for n in range(3)]
            moments = [(sb(ph, f"pair{n}", [P, T, 2]), sb(ph, f"dif{n}", [P, T]), sb(ph, f"var{n}", [P, T]))
                       for n in range(3)]
            veps = [sb(ph, f"veps{n}", [P, T]) for n in range(3)]
            nmean = [sb(ph, f"nmean{n}", [P, T]) for n in range(3)]
            rstd = [sb(ph, f"rstd{n}", [P, T]) for n in range(3)]
            nmr = [sb(ph, f"nmr{n}", [P, T]) for n in range(3)]

            pT = ph.enter_context(nc.psum_tensor("pT2", [P, C, N], F32))
            pH = ph.enter_context(nc.psum_tensor("pH", [P, 4, N], F32))
            pO = ph.enter_context(nc.psum_tensor("pO2", [P, 2, N], F32))

            (s_x, s_res, s_out, x1_done, x1Tp, x1h_done, x1l_done, h_mm, g_done, hh_done, hl_done, r_done,
             o_mm, r2_done, x2_done, x2Tp, x2h_done, x2l_done, u_mm, u_done, uh_done, ul_done, x2b_done,
             f_mm, z_done, o_done) = sem(
                ph, "s_x", "s_res", "s_out", "x1_done", "x1Tp", "x1h_done", "x1l_done", "h_mm", "g_done",
                "hh_done", "hl_done", "r_done", "o_mm2", "r2_done", "x2_done", "x2Tp", "x2h_done",
                "x2l_done", "u_mm", "u_done", "uh_done", "ul_done", "x2b_done", "f_mm", "z_done", "o_done")
            stats_done = sem(ph, "stats1", "stats2", "stats3")
            levels = sem(ph, "levels1", "levels2", "levels3")
            moments_done = sem(ph, "moments1", "moments2", "moments3")
            scale_done = sem(ph, "scale1", "scale2", "scale3")
            norm_done = [x1_done, x2_done, o_done]
            HEAD = 6

            block = ph.enter_context(nc.Block())

            def rows_of(dram, j):
                return dram[j * P:(j + 1) * P, :] if isinstance(j, int) else dram[bass.ds(j * P, P), :]

            @block.sync
            def _(sp):
                sp.dma_start(x_in[:], rows_of(x_dram, 0)).then_inc(s_x, 16)
                sp.dma_start(r_sb[:], rows_of(src_rows, 0)).then_inc(s_res, 16)

                def step(i, ahead):
                    if exists(i, 1):
                        sp.wait_ge(o_done, T * i)
                        sp.dma_start(rows_of(out_rows, i - 1), o_sb[:]).then_inc(s_out, 16)
                    if ahead:
                        sp.wait_ge(r_done, 2 * (i + 2))
                        sp.dma_start(x_in[:], rows_of(x_dram, i + 2)).then_inc(s_x, 16)
                        sp.wait_ge(r2_done, 2 * (i + 2))
                        sp.dma_start(r_sb[:], rows_of(src_rows, i + 2)).then_inc(s_res, 16)

                step(-1, True)
                step(0, True)
                with sp.Fori(1, S - 2) as i:
                    step(i, True)
                step(S - 2, False)
                step(S - 1, False)
                step(S, False)
                sp.wait_ge(s_out, 16 * S)

            @block.gpsimd
            def _(pool):
                def scale(n, j):
                    finish_scale(pool, veps[n], nmean[n], rstd[n], nmr[n], moments_done[n], scale_done[n],
                                 norm_done[n], j)

                scale(0, 0)

                def step(i, back, front, ahead):
                    if exists(i, 1):
                        scale(2, i - 1)
                    if front:
                        pool.wait_ge(s_res, 16 * (i + 2))
                        pool.wait_ge(s_x, 16 * (i + 2))
                        nc.gpsimd.tensor_tensor(r_sb[:], r_sb[:], x_in[:], ALU.add).then_inc(r_done, 1)
                        pool.wait_ge(r_done, 2 * (i + 1) + 1)
                        pool.wait_ge(x1_done, T * (i + 2))
                        nc.gpsimd.tensor_tensor(r_sb[:], r_sb[:],
                                                row_b2[:].rearrange("p (o d) -> p o d", o=1).broadcast_to([P, T, D]),
                                                ALU.add).then_inc(r_done, 1)
                    if back:
                        if exists(i, 1):
                            pool.wait_ge(z_done, 2 * i)
                        pool.wait_ge(x2_done, T * (i + 1))
                        nc.gpsimd.tensor_tensor(x2b[:], x2[:],
                                                row_fb2[:].rearrange("p (o d) -> p o d", o=1).broadcast_to([P, T, D]),
                                                ALU.add).then_inc(x2b_done, 1)
                    if ahead:
                        scale(0, i + 2)
                    if back:
                        for m in range(M):
                            pool.wait_ge(uh_done, M * i + m + 1)
                            nc.gpsimd.tensor_tensor(uT[1][:, m], u_sb[:, m % RELU_SLOTS],
                                                    uT[0][:, m].bitcast(F32), ALU.subtract).then_inc(ul_done, 1)
                    if front:
                        scale(1, i + 1)

                step(-1, False, True, True)
                step(0, True, True, True)
                with pool.Fori(1, S - 2) as i:
                    step(i, True, True, True)
                step(S - 2, True, True, False)
                step(S - 1, True, False, False)
                step(S, False, False, False)

            @block.scalar
            def _(act):
                def split(j, ps_ready, done, parts):
                    for c in range(C):
                        act.wait_ge(ps_ready, 2 * j + c + 1)
                        nc.scalar.activation(parts[0][:, c], pT[:, c], ACT.Copy).then_inc(done, 1)

                def normalise(n, j, source, result, tiles=range(T)):
                    act.wait_ge(scale_done[n], 2 * j + 2)
                    for t in tiles:
                        nc.scalar.activation(result[:, t], source[:, t], ACT.Identity, bias=nmr[n][:, t:t + 1],
                                             scale=rstd[n][:, t:t + 1]).then_inc(norm_done[n], 1)

                def gelu(j, m):
                    if m >= 3:
                        act.wait_ge(hl_done, M * j + m - 2)
                    elif exists(j, 1):
                        act.wait_ge(hl_done, M * j)
                    act.wait_ge(h_mm, M * j + m + 1)
                    nc.scalar.activation(g_sb[:, m % 3], pH[:, m % 4], ACT.Gelu, bias=b1c[:, m:m + 1]).then_inc(g_done, 1)

                act.wait_ge(s_x, 16)
                normalise(0, 0, x_in, x1)
                split(0, x1Tp, x1h_done, x1T)

                def step(i, back, front, ahead):
                    if front:
                        for m in range(HEAD):
                            gelu(i + 1, m)
                            if m in (3, 5) and exists(i, 1):
                                norm_out(i, (0, 1) if m == 3 else (2, 3))
                    elif exists(i, 1):
                        norm_out(i, range(T))
                    if back:
                        split(i, x2Tp, x2h_done, x2T)
                    if front:
                        for m in range(HEAD, M):
                            gelu(i + 1, m)
                    if back:
                        for m in range(M):
                            act.wait_ge(u_mm, M * i + m + 1)
                            if m >= RELU_SLOTS:
                                act.wait_ge(ul_done, M * i + m - RELU_SLOTS + 1)
                            elif exists(i, 1):
                                act.wait_ge(ul_done, M * i)
                            nc.scalar.activation(u_sb[:, m % RELU_SLOTS], pH[:, m % 4], ACT.Relu,
                                                 bias=cols[:, COL_FB1 + m:COL_FB1 + m + 1]).then_inc(u_done, 1)
                    if ahead:
                        norm_x(i)
                        split(i + 2, x1Tp, x1h_done, x1T)
                    if front:
                        if exists(i, 0):
                            act.wait_ge(x2Tp, 2 * (i + 1))
                            act.wait_ge(x2b_done, i + 1)
                        normalise(1, i + 1, r2, x2)

                def norm_out(i, tiles):
                    if exists(i, 2):
                        act.wait_ge(s_out, 16 * (i - 1))
                    normalise(2, i - 1, z_sb, o_sb, tiles)

                def norm_x(i):
                    act.wait_ge(x1Tp, 2 * (i + 2))
                    act.wait_ge(s_x, 16 * (i + 3))
                    normalise(0, i + 2, x_in, x1)

                step(-1, False, True, True)
                step(0, True, True, True)
                with act.Fori(1, S - 2) as i:
                    step(i, True, True, True)
                step(S - 2, True, True, False)
                step(S - 1, True, False, False)
                step(S, False, False, False)

            @block.vector
            def _(dve):
                def stats(n, j, tile, t):
                    nc.vector.bn_stats(bn[n][:, t], tile[:, t]).then_inc(stats_done[n], 1)

                def aggregate(n, j):
                    for level in range(4):
                        moments_level(level, dve, bn[n], stats_done[n], levels[n], moments[n], (veps[n], nmean[n]),
                                      moments_done[n], scale_done[n], j)

                def x_stats(j):
                    dve.wait_ge(s_x, 16 * (j + 1))
                    for t in range(T):
                        stats(0, j, x_in, t)
                    aggregate(0, j)

                def split(j, hi_done, done, parts):
                    for c in range(C):
                        dve.wait_ge(hi_done, 2 * j + c + 1)
                        nc.vector.tensor_tensor(parts[1][:, c], pT[:, c], parts[0][:, c].bitcast(F32),
                                                ALU.subtract).then_inc(done, 1)

                def split_gelu(j, m):
                    dve.wait_ge(g_done, M * j + m + 1)
                    nc.vector.tensor_copy(hT[0][:, m], g_sb[:, m % 3]).then_inc(hh_done, 1)
                    dve.wait_ge(hh_done, M * j + m + 1)
                    nc.vector.tensor_tensor(hT[1][:, m], g_sb[:, m % 3], hT[0][:, m].bitcast(F32),
                                            ALU.subtract).then_inc(hl_done, 1)

                x_stats(0)
                split(0, x1h_done, x1l_done, x1T)

                def step(i, back, front, ahead):
                    if front:
                        for m in range(HEAD):
                            split_gelu(i + 1, m)
                    if back:
                        split(i, x2h_done, x2l_done, x2T)
                    if front:
                        for m in range(HEAD, M):
                            split_gelu(i + 1, m)
                    if ahead:
                        x_stats(i + 2)
                    if back:
                        for m in range(M):
                            dve.wait_ge(u_done, M * i + m + 1)
                            nc.vector.tensor_copy(uT[0][:, m], u_sb[:, m % RELU_SLOTS]).then_inc(uh_done, 1)
                    if front:
                        for h in range(2):
                            if h == 0:
                                dve.wait_ge(r_done, 2 * (i + 2))
                                if exists(i, 0):
                                    dve.wait_ge(x2_done, T * (i + 1))
                            dve.wait_ge(o_mm, 2 * (i + 1) + h + 1)
                            nc.vector.tensor_tensor(r2[:, 2 * h:2 * h + 2], pO[:, h].rearrange("p (t d) -> p t d", t=2),
                                                    r_sb[:, 2 * h:2 * h + 2], ALU.add).then_inc(r2_done, 1)
                            dve.wait_ge(r2_done, 2 * (i + 1) + h + 1)
                            for t in (2 * h, 2 * h + 1):
                                stats(1, i + 1, r2, t)
                            if h == 0 and ahead:
                                split(i + 2, x1h_done, x1l_done, x1T)
                        aggregate(1, i + 1)
                    if back:
                        for h in range(2):
                            if h == 0:
                                dve.wait_ge(x2b_done, i + 1)
                                if exists(i, 1):
                                    dve.wait_ge(o_done, T * i)
                            dve.wait_ge(f_mm, 2 * i + h + 1)
                            nc.vector.tensor_tensor(z_sb[:, 2 * h:2 * h + 2],
                                                    pO[:, h].rearrange("p (t d) -> p t d", t=2),
                                                    x2b[:, 2 * h:2 * h + 2], ALU.add).then_inc(z_done, 1)
                            dve.wait_ge(z_done, 2 * i + h + 1)
                            for t in (2 * h, 2 * h + 1):
                                stats(2, i, z_sb, t)
                        aggregate(2, i)

                step(-1, False, True, True)
                step(0, True, True, True)
                with dve.Fori(1, S - 2) as i:
                    step(i, True, True, True)
                step(S - 2, True, True, False)
                step(S - 1, True, False, False)

            @block.tensor
            def _(pe):
                def transposes(src_tile, ready):
                    for c in range(C):
                        for t in range(T):
                            mm = nc.tensor.transpose(pT[:, c, t * P:(t + 1) * P], src_tile[:, t, c * P:(c + 1) * P],
                                                     ident[:])
                        mm.then_inc(ready, 1)

                def mlp_up(j, m):
                    if m >= 4:
                        pe.wait_ge(g_done, M * j + m - 3)
                    for n, (a, w) in enumerate(passes3):
                        for c in range(C):
                            mm = nc.tensor.matmul(pH[:, m % 4], w1s[w][:, c, m * P:(m + 1) * P], x1T[a][:, c],
                                                  start=n == 0 and c == 0, stop=n == 2 and c == C - 1)
                    mm.then_inc(h_mm, 1)

                pe.wait_ge(x1_done, T)
                transposes(x1, x1Tp)

                def step(i, back, front, ahead):
                    if front:
                        pe.wait_ge(x1h_done, 2 * (i + 2))
                        pe.wait_ge(x1l_done, 2 * (i + 2))
                        for m in range(HEAD):
                            mlp_up(i + 1, m)
                    if back:
                        pe.wait_ge(x2_done, T * (i + 1))
                        transposes(x2, x2Tp)
                    if front:
                        for m in range(HEAD, M):
                            mlp_up(i + 1, m)
                    if back:
                        pe.wait_ge(x2h_done, 2 * (i + 1))
                        pe.wait_ge(x2l_done, 2 * (i + 1))
                        for m in range(M):
                            if m < 4 and front:
                                pe.wait_ge(g_done, M * (i + 1) + m + 5)
                            if m >= 4:
                                pe.wait_ge(u_done, M * i + m - 3)
                            for a in range(2):
                                for c in range(C):
                                    mm = nc.tensor.matmul(pH[:, m % 4], fq1[:, c, m * P:(m + 1) * P], x2T[a][:, c],
                                                          start=a == 0 and c == 0, stop=a == 1 and c == C - 1)
                            mm.then_inc(u_mm, 1)
                    if front:
                        pe.wait_ge(hh_done, M * (i + 2))
                        pe.wait_ge(hl_done, M * (i + 2))
                        for t in range(T):
                            if t == 2 and ahead:
                                pe.wait_ge(x1_done, T * (i + 3))
                                transposes(x1, x1Tp)
                            if t % 2 == 0 and exists(i, 1):
                                pe.wait_ge(z_done, 2 * (i - 1) + t // 2 + 1)
                            for n, (a, w) in enumerate(passes3):
                                for m in range(M):
                                    mm = nc.tensor.matmul(pO[:, t // 2, t % 2 * D:(t % 2 + 1) * D],
                                                          hT[a][:, m, t * P:(t + 1) * P], w2s[w][:, m],
                                                          start=n == 0 and m == 0, stop=n == 2 and m == M - 1)
                            if t % 2:
                                mm.then_inc(o_mm, 1)
                    if back:
                        pe.wait_ge(uh_done, M * (i + 1))
                        pe.wait_ge(ul_done, M * (i + 1))
                        for t in range(T):
                            if t % 2 == 0 and front:
                                pe.wait_ge(r2_done, 2 * (i + 1) + t // 2 + 1)
                            elif t % 2 == 0:
                                pe.wait_ge(z_done, 2 * (i - 1) + t // 2 + 1)
                            for a in range(2):
                                for m in range(M):
                                    mm = nc.tensor.matmul(pO[:, t // 2, t % 2 * D:(t % 2 + 1) * D],
                                                          uT[a][:, m, t * P:(t + 1) * P], fq2[:, m],
                                                          start=a == 0 and m == 0, stop=a == 1 and m == M - 1)
                            if t % 2:
                                mm.then_inc(f_mm, 1)

                step(-1, False, True, True)
                step(0, True, True, True)
                with pe.Fori(1, S - 2) as i:
                    step(i, True, True, True)
                step(S - 2, True, True, False)
                step(S - 1, True, False, False)


def kernel(L0_attn_src, L0_attn_qkv_w, L0_attn_qkv_b, L0_attn_out_w, L0_attn_out_b, L0_attn_w1, L0_attn_b1,
           L0_attn_w2, L0_attn_b2, L0_attn_g1, L0_attn_be1, L0_attn_g2, L0_attn_be2, L0_ffn_W1, L0_ffn_b1,
           L0_ffn_W2, L0_ffn_b2):
    import numpy as np
    import concourse.bacc as bacc
    from concourse.bass_utils import run_bass_kernel_spmd

    def column(v):
        return np.asarray(v).reshape(-1, P).T

    qkv_b = np.asarray(L0_attn_qkv_b)
    cols = np.concatenate([column(v) for v in (L0_attn_g1, L0_attn_be1, L0_attn_g2, L0_attn_be2, qkv_b[:D],
                                               L0_attn_b1, L0_ffn_b1)], axis=1)
    rows = np.concatenate([qkv_b[D:], np.asarray(L0_attn_out_b), np.asarray(L0_attn_b2), np.asarray(L0_ffn_b2)])
    head = np.arange(P) // HD
    const = np.concatenate([np.eye(P), head[:, None] == head[None, :], head[:, None] == np.arange(HC)[None, :]],
                           axis=1).astype(np.float32)
    arrays = {
        "src": L0_attn_src, "qkv_w": L0_attn_qkv_w, "out_w": L0_attn_out_w, "w1": L0_attn_w1, "w2": L0_attn_w2,
        "fw1": np.asarray(L0_ffn_W1).T, "fw2": np.asarray(L0_ffn_W2).T, "cols": cols, "rows": rows[None, :],
        "const": const,
    }
    arrays = {name: np.ascontiguousarray(a) for name, a in arrays.items()}
    nc = bacc.Bacc("TRN2", target_bir_lowering=False, num_devices=1)
    args = [nc.dram_tensor(name + "_dram", a.shape, mybir.dt.from_np(a.dtype), kind="ExternalInput").ap()
            for name, a in arrays.items()]
    out = nc.dram_tensor("out_dram", (S, N, D), F32, kind="ExternalOutput").ap()
    build(nc, *args, out)
    r = run_bass_kernel_spmd(nc, [{name + "_dram": a for name, a in arrays.items()}], core_ids=[0])
    return r.results[0]["out_dram"]
```

```python
from contextlib import ExitStack

import concourse.bass as bass
from concourse import mybir

P = 128
D = 256
F = 1024
S = 16
N = 512
T = N // P
C = D // P
M = F // P
HEADS = 16
HD = D // HEADS
HC = P // HD
VW = P + 2
KW = P + HC
LN_EPS = 1e-5
ATTN_EPS = 1e-6
Q_EPS = 1e-5

F32 = mybir.dt.float32
F32R = mybir.dt.float32r
ALU = mybir.AluOpType
ACT = mybir.ActivationFunctionType
AX = mybir.AxisListType

COL_G1, COL_BE1, COL_G2, COL_BE2, COL_BQ, COL_B1, COL_FB1, COLS = 0, 2, 4, 6, 8, 10, 18, 26
LN_SRC, LN_X, LN_R, LN_Z = range(4)
ROW_KV, ROW_OUT, ROW_B2, ROW_FB2, ROWS = 0, 512, 768, 1024, 1280


def exists(i, back):
    return not isinstance(i, int) or i >= back


def build(nc, src, qkv_w, out_w, w1, w2, fw1, fw2, cols_in, rows_in, const_in, out):
    src_rows = src.rearrange("s (p t) d -> (s p) (t d)", t=T)
    out_rows = out.rearrange("s (p t) d -> (s p) (t d)", t=T)
    x_dram = nc.dram_tensor("x_dram", (S * P, T * D), F32, kind="Internal").ap()

    with ExitStack() as whole:
        def sb(stack, name, shape, dt=F32):
            return stack.enter_context(nc.sbuf_tensor(name, shape, dt))

        def sem(*names):
            return [whole.enter_context(nc.semaphore(n)) for n in names]

        wqkv = [sb(whole, f"wqkv_{k}", [P, C, 3 * D], F32R) for k in "hl"]
        wout = [sb(whole, f"wout_{k}", [P, C, D], F32R) for k in "hl"]
        w1s = [sb(whole, f"w1_{k}", [P, C, F], F32R) for k in "hl"]
        w2s = [sb(whole, f"w2_{k}", [P, M, D], F32R) for k in "hl"]
        fq1 = sb(whole, "fq1", [P, C, F], F32R)
        fq2 = sb(whole, "fq2", [P, M, D], F32R)
        cols = sb(whole, "cols", [P, COLS])
        ident = sb(whole, "ident", [P, P])
        b1c = sb(whole, "b1c", [P, M])
        row_b2 = sb(whole, "row_b2", [P, D])
        row_fb2 = sb(whole, "row_fb2", [P, D])
        half4 = sb(whole, "half4", [P, T])
        minus1 = sb(whole, "minus1", [P, 1])
        warm = sb(whole, "warm", [P, 1])
        bn = [sb(whole, f"bn{n}", [P, T, 6]) for n in range(4)]
        moments = [(sb(whole, f"pair{n}", [P, T, 2]), sb(whole, f"dif{n}", [P, T]), sb(whole, f"var{n}", [P, T]))
                   for n in range(4)]
        veps = [sb(whole, f"veps{n}", [P, T]) for n in range(4)]
        nmean = [sb(whole, f"nmean{n}", [P, T]) for n in range(4)]
        rstd = [sb(whole, f"rstd{n}", [P, T]) for n in range(4)]
        nmr = [sb(whole, f"nmr{n}", [P, T]) for n in range(4)]

        with ExitStack() as ph:
            qkv_raw = sb(ph, "qkv_raw", [P, C, 3 * D])
            out_raw = sb(ph, "out_raw", [P, C, D])
            w1_raw = sb(ph, "w1_raw", [P, C, F])
            w2_raw = sb(ph, "w2_raw", [P, M, D])
            w_scaled = sb(ph, "w_scaled", [P, C * F])
            below = sb(ph, "below", [P, C * F])
            f1_raw = sb(ph, "f1_raw", [P, C, F])
            f2_raw = sb(ph, "f2_raw", [P, M, D])
            rows_kv = sb(ph, "rows_kv", [P, 2 * D])
            row_v = sb(ph, "row_v", [P, D])
            be1_wide = sb(ph, "be1_wide", [P, C, P])
            mask = sb(ph, "mask", [P, KW])
            ones = sb(ph, "ones", [P, P])
            row_k1 = sb(ph, "row_k1", [P, D])
            row_out = sb(ph, "row_out", [P, D])
            bv_mask = sb(ph, "bv_mask", [P, C, P])
            bq_neg = sb(ph, "bq_neg", [P, C])
            bq_one = sb(ph, "bq_one", [P, C])
            abs_sum = sb(ph, "abs_sum", [P, 2, 8])
            abs_tot = sb(ph, "abs_tot", [P, 2])
            thr = sb(ph, "thr", [P, 2])
            thr_neg = sb(ph, "thr_neg", [P, 2])

            src_sb = sb(ph, "src_sb", [P, 2, T, D])
            srcb = sb(ph, "srcb", [P, 2, T, D])
            xhat = sb(ph, "xhat", [P, T, D])
            xT = [sb(ph, f"xT_{k}", [P, C, N], F32R) for k in "hl"]
            k1 = sb(ph, "k1", [P, T, D])
            ek = sb(ph, "ek", [P, T, D])
            kf = sb(ph, "kf", [P, T, D])
            v_sb = sb(ph, "v_sb", [P, T, C, VW])
            eq = sb(ph, "eq", [P, C, N])
            qf = sb(ph, "qf", [P, C, N])
            kvm = sb(ph, "kvm", [P, C, P])
            kvz = sb(ph, "kvz", [P, C, KW])
            den = sb(ph, "den", [P, 2, 2 * C, HC])
            rden = sb(ph, "rden", [P, 2, 2 * C, HC])
            y_sb = sb(ph, "y_sb", [P, T, D])
            yT = [sb(ph, f"yT_{k}", [P, C, N], F32R) for k in "hl"]
            x_sb = sb(ph, "x_sb", [P, T, D])

        with ExitStack() as ph:
            x_in = sb(ph, "x_in", [P, T, D])
            r_sb = sb(ph, "r_sb", [P, T, D])
            x1 = sb(ph, "x1", [P, T, D])
            x1T = [sb(ph, f"x1T_{k}", [P, C, N], F32R) for k in "hl"]
            g_sb = sb(ph, "g_sb", [P, 3, N])
            hT = [sb(ph, f"hT_{k}", [P, M, N], F32R) for k in "hl"]
            z_sb = sb(ph, "z_sb", [P, T, D])
            RELU_SLOTS = 6
            u_sb = sb(ph, "u_sb", [P, RELU_SLOTS, N])
            uT = [sb(ph, f"uT_{k}", [P, M, N], F32R) for k in "hl"]
            r2 = sb(ph, "r2", [P, T, D])
            x2 = sb(ph, "x2", [P, T, D])
            x2b = sb(ph, "x2b", [P, T, D])
            x2T = [sb(ph, f"x2T_{k}", [P, C, N], F32R) for k in "hl"]
            o_sb = sb(ph, "o_sb", [P, T, D])

        pT = whole.enter_context(nc.psum_tensor("pT", [P, C, N], F32))
        pH = whole.enter_context(nc.psum_tensor("pH", [P, 4, N], F32))
        pO = whole.enter_context(nc.psum_tensor("pO", [P, 2, N], F32))
        pKV = pH[:, 0:2]
        pQ = pH[:, 2:4]
        pS = pO[:, 0]
        pA = pO[:, 1]

        (s_vec, s_wqkv, s_wout, s_wmlp, s_wffn, s_const, s_src0, s_src1, s_stored, s_x, s_res, s_out) = sem(
            "s_vec", "s_wqkv", "s_wout", "s_wmlp", "s_wffn", "s_const", "s_src0", "s_src1", "s_stored",
            "s_x", "s_res", "s_out")
        s_rows, s_rows_kv, s_rows_out, s_mask = sem("s_rows", "s_rows_kv", "s_rows_out", "s_mask")
        s_src = [s_src0, s_src1]
        (setup_dve, setup_act, setup_pe_mm, b1_mm, thr_mm, scaled, wsplit, w1_scaled, w_hi, w_lo, brow_done,
         bq_done, b1c_done, abs_done, thr_done, below_done, tern_done) = sem(
            "setup_dve", "setup_act", "setup_pe_mm", "b1_mm", "thr_mm", "scaled", "wsplit", "w1_scaled", "w_hi",
            "w_lo", "brow_done", "bq_done", "b1c_done", "abs_done", "thr_done", "below_done", "tern_done")
        stats_done = sem("stats0", "stats1", "stats2", "stats3")
        levels = sem("levels0", "levels1", "levels2", "levels3")
        moments_done = sem("moments0", "moments1", "moments2", "moments3")
        scale_done = sem("scale0", "scale1", "scale2", "scale3")
        norm_done = sem("xhat_done", "x1_done", "x2_done", "out_done")
        xhat_done, x1_done, x2_done, out_done = norm_done
        (srcb_done, xTp, xh_done, xl_done, kv_mm, k1_done, v_done, ek_done, kf_done, q_mm, rq_done, eq_done,
         qf_done, s_mm, kvm_done, kvz_done, num_mm, den_done, rden_done, y_done, yTp, yh_done, yl_done, o_mm,
         x_done) = sem(
            "srcb_done", "xTp", "xh_done", "xl_done", "kv_mm", "k1_done", "v_done", "ek_done", "kf_done", "q_mm",
            "rq_done", "eq_done", "qf_done", "s_mm", "kvm_done", "kvz_done", "num_mm", "den_done", "rden_done",
            "y_done", "yTp", "yh_done", "yl_done", "o_mm", "x_done")
        (x1Tp, x1h_done, x1l_done, h_mm, g_done, hh_done, hl_done, r_done, w2_mm, r2_done, x2Tp, x2h_done,
         x2l_done, u_mm, u_done, uh_done, ul_done, ul_odd, x2b_done, f_mm, z_done) = sem(
            "x1Tp", "x1h_done", "x1l_done", "h_mm", "g_done", "hh_done", "hl_done", "r_done", "w2_mm", "r2_done",
            "x2Tp", "x2h_done", "x2l_done", "u_mm", "u_done", "uh_done", "ul_done", "ul_odd", "x2b_done", "f_mm", "z_done")

        passes3 = [(0, 0), (0, 1), (1, 0)]
        FIRST, LAST = 5, 11
        THR = 2 * VW + 40
        HEAD = 6

        def last_low(m):
            return (ul_odd, m // 2 + 1) if m % 2 else (ul_done, M * (S - 1) + m // 2 + 1)

        def rows_of(dram, j):
            return dram[j * P:(j + 1) * P, :] if isinstance(j, int) else dram[bass.ds(j * P, P), :]

        def moments_level(level, dve, n, j):
            pair, dif, var = moments[n]
            if level == 0:
                dve.wait_ge(stats_done[n], T * j + T)
                nc.vector.tensor_tensor(pair[:], bn[n][:, :, 1:3], bn[n][:, :, 4:6], ALU.add).then_inc(levels[n], 1)
                nc.vector.tensor_tensor(dif[:], bn[n][:, :, 1], bn[n][:, :, 4], ALU.subtract).then_inc(levels[n], 1)
            if level == 1:
                if exists(j, 1):
                    dve.wait_ge(scale_done[n], 2 * j)
                dve.wait_ge(levels[n], 4 * j + 1)
                nc.vector.tensor_scalar(nmean[n][:], pair[:, :, 0], -0.5, None, ALU.mult).then_inc(moments_done[n], 1)
                dve.wait_ge(levels[n], 4 * j + 2)
                nc.vector.scalar_tensor_tensor(out=dif[:], in0=dif[:], scalar=0.25, in1=dif[:], op0=ALU.mult,
                                               op1=ALU.mult).then_inc(levels[n], 1)
            if level == 2:
                dve.wait_ge(levels[n], 4 * j + 3)
                nc.vector.scalar_tensor_tensor(out=var[:], in0=pair[:, :, 1], scalar=1.0 / D, in1=dif[:],
                                               op0=ALU.mult, op1=ALU.add).then_inc(levels[n], 1)
            if level == 3:
                dve.wait_ge(levels[n], 4 * j + 4)
                nc.vector.tensor_scalar(veps[n][:], var[:], LN_EPS, None, ALU.add).then_inc(moments_done[n], 1)

        def scale(pool, n, j):
            if exists(j, 1):
                pool.wait_ge(norm_done[n], T * j)
            pool.wait_ge(moments_done[n], 2 * j + 2)
            nc.gpsimd.tensor_tensor(rstd[n][:], veps[n][:], half4[:], ALU.pow).then_inc(scale_done[n], 1)
            pool.wait_ge(scale_done[n], 2 * j + 1)
            nc.gpsimd.tensor_tensor(nmr[n][:], nmean[n][:], rstd[n][:], ALU.mult).then_inc(scale_done[n], 1)

        block = whole.enter_context(nc.Block())

        def src_landed(engine, j, slot):
            engine.wait_ge(s_src[slot], 16 * (j // 2 + 1) if isinstance(j, int) else j * 8 + (8 if slot else 16))

        @block.sync
        def _(sp):
            sp.dma_start(src_sb[:, 0], src_rows[0:P, :]).then_inc(s_src[0], 16)
            sp.dma_start(ident[:], const_in[:, 0:P]).then_inc(s_const, 16)
            sp.dma_start(rows_kv[:], rows_in[:, ROW_KV:ROW_KV + 2 * D].broadcast_to([P, 2 * D])).then_inc(s_rows_kv, 16)
            sp.dma_start(src_sb[:, 1], src_rows[P:2 * P, :]).then_inc(s_src[1], 16)
            sp.dma_start(row_out[:], rows_in[:, ROW_OUT:ROW_OUT + D].broadcast_to([P, D])).then_inc(s_rows_out, 16)
            sp.dma_start(mask[:], const_in[:, P:P + KW]).then_inc(s_mask, 16)
            sp.dma_start(out_raw[:], out_w.rearrange("(c p) n -> p c n", p=P)).then_inc(s_wout, 16)
            sp.dma_start(w1_raw[:], w1.rearrange("(c p) n -> p c n", p=P)).then_inc(s_wmlp, 16)
            sp.dma_start(w2_raw[:], w2.rearrange("(m p) n -> p m n", p=P)).then_inc(s_wmlp, 16)
            sp.dma_start(f1_raw[:], fw1.rearrange("(c p) n -> p c n", p=P)).then_inc(s_wffn, 16)
            sp.dma_start(f2_raw[:], fw2.rearrange("(m p) n -> p m n", p=P)).then_inc(s_wffn, 16)
            sp.dma_start(row_b2[:], rows_in[:, ROW_B2:ROW_B2 + D].broadcast_to([P, D])).then_inc(s_rows, 16)
            sp.dma_start(row_fb2[:], rows_in[:, ROW_FB2:ROW_FB2 + D].broadcast_to([P, D])).then_inc(s_rows, 16)

            def attention_step(i, slot, more):
                if more:
                    sp.wait_ge(srcb_done, i + 1)
                    sp.wait_ge(xhat_done, T * i + T)
                    sp.dma_start(src_sb[:, slot], rows_of(src_rows, i + 2)).then_inc(s_src[slot], 16)
                if exists(i, 1):
                    sp.wait_ge(x_done, 2 * i)
                    sp.dma_start(rows_of(x_dram, i - 1), x_sb[:]).then_inc(s_stored, 16)

            for i in range(FIRST):
                attention_step(i, i % 2, True)
            with sp.Fori(FIRST, LAST, 2) as i:
                attention_step(i, 1, True)
                attention_step(i + 1, 0, True)
            for i in range(LAST, S - 2):
                attention_step(i, i % 2, True)
            sp.wait_ge(s_stored, 16 * (S - 3))
            sp.wait_ge(w_lo, 2)
            sp.dma_start(x_in[:], rows_of(x_dram, 0)).then_inc(s_x, 16)
            sp.dma_start(r_sb[:], rows_of(src_rows, 0)).then_inc(s_res, 16)
            attention_step(S - 2, 0, False)
            attention_step(S - 1, 1, False)

            def load_x(j):
                sp.wait_ge(r_done, 2 * j)
                sp.dma_start(x_in[:], rows_of(x_dram, j)).then_inc(s_x, 16)

            def load_residual(j):
                sp.wait_ge(r2_done, 2 * j)
                sp.dma_start(r_sb[:], rows_of(src_rows, j)).then_inc(s_res, 16)

            def mlp_step(i, ahead):
                if ahead:
                    load_x(i + 2)
                if exists(i, 1):
                    sp.wait_ge(out_done, T * i)
                    sp.dma_start(rows_of(out_rows, i - 1), o_sb[:]).then_inc(s_out, 16)
                if ahead:
                    load_residual(i + 2)

            load_x(1)
            attention_step(S, 0, False)
            load_residual(1)
            sp.wait_ge(s_stored, 16 * S)
            mlp_step(0, True)
            with sp.Fori(1, S - 2) as i:
                mlp_step(i, True)
            mlp_step(S - 2, False)
            mlp_step(S - 1, False)
            mlp_step(S, False)
            sp.wait_ge(s_out, 16 * S)

        @block.gpsimd
        def _(pool):
            pool.memset(minus1[:], -1.0).then_inc(setup_act, 1)
            pool.memset(half4[:], -0.5).then_inc(setup_act, 1)
            pool.memset(v_sb[:, :, :, P:VW], 1.0).then_inc(setup_act, 1)
            pool.wait_ge(setup_act, 3)

            def add_bias(j, slot):
                if exists(j, 2):
                    pool.wait_ge(x_done, 2 * j - 2)
                src_landed(pool, j, slot)
                for t in range(T):
                    last = nc.gpsimd.tensor_tensor(srcb[:, slot, t], src_sb[:, slot, t], row_out[:], ALU.add)
                last.then_inc(srcb_done, 1)

            def low_part(raw, parts, n):
                pool.wait_ge(w_hi, n + 1)
                nc.gpsimd.tensor_tensor(parts[1][:].rearrange("p a b -> p (a b)"), raw,
                                        parts[0][:].bitcast(F32).rearrange("p a b -> p (a b)"),
                                        ALU.subtract).then_inc(w_lo, 1)

            def attention_step(i, slot):
                scale(pool, LN_SRC, i + 2)
                add_bias(i + 1, 1 - slot)

            scale(pool, LN_SRC, 0)
            pool.wait_ge(s_rows_out, 16)
            add_bias(0, 0)
            scale(pool, LN_SRC, 1)
            for i in range(FIRST):
                attention_step(i, i % 2)
                if i == 2:
                    low_part(w_scaled[:], w1s, 0)
                if i == 3:
                    low_part(w2_raw[:].rearrange("p a b -> p (a b)"), w2s, 1)
            with pool.Fori(FIRST, LAST, 2) as i:
                attention_step(i, 1)
                attention_step(i + 1, 0)
            for i in range(LAST, S - 2):
                attention_step(i, i % 2)
            scale(pool, LN_X, 0)
            add_bias(S - 1, 1)

            def mlp_step(i, back, front, ahead):
                if exists(i, 1):
                    scale(pool, LN_Z, i - 1)
                if front:
                    pool.wait_ge(s_res, 16 * (i + 2))
                    pool.wait_ge(s_x, 16 * (i + 2))
                    nc.gpsimd.tensor_tensor(r_sb[:], r_sb[:], x_in[:], ALU.add).then_inc(r_done, 1)
                    pool.wait_ge(r_done, 2 * (i + 1) + 1)
                    pool.wait_ge(x1_done, T * (i + 2))
                    nc.gpsimd.tensor_tensor(r_sb[:], r_sb[:],
                                            row_b2[:].rearrange("p (o d) -> p o d", o=1).broadcast_to([P, T, D]),
                                            ALU.add).then_inc(r_done, 1)
                if back:
                    if exists(i, 1):
                        pool.wait_ge(z_done, 2 * i)
                    pool.wait_ge(x2_done, T * (i + 1))
                    nc.gpsimd.tensor_tensor(x2b[:], x2[:],
                                            row_fb2[:].rearrange("p (o d) -> p o d", o=1).broadcast_to([P, T, D]),
                                            ALU.add).then_inc(x2b_done, 1)
                if ahead:
                    scale(pool, LN_X, i + 2)
                if back:
                    for m in range(0, M, 1 if front else 2):
                        pool.wait_ge(uh_done, M * i + m + 1)
                        nc.gpsimd.tensor_tensor(uT[1][:, m], u_sb[:, m % RELU_SLOTS],
                                                uT[0][:, m].bitcast(F32), ALU.subtract).then_inc(ul_done, 1)
                if front:
                    scale(pool, LN_R, i + 1)

            pool.wait_ge(s_rows, 32)
            mlp_step(-1, False, True, True)
            mlp_step(0, True, True, True)
            with pool.Fori(1, S - 2) as i:
                mlp_step(i, True, True, True)
            mlp_step(S - 2, True, True, False)
            mlp_step(S - 1, True, False, False)
            mlp_step(S, False, False, False)

        @block.scalar
        def _(act):
            act.dma_start(cols[:], cols_in).then_inc(s_vec, 16)
            act.dma_start(qkv_raw[:], qkv_w.rearrange("(c p) n -> p c n", p=P)).then_inc(s_wqkv, 16)

            def split(j, ps_ready, done, parts):
                for c in range(C):
                    act.wait_ge(ps_ready, 2 * j + c + 1)
                    nc.scalar.activation(parts[0][:, c], pT[:, c], ACT.Copy).then_inc(done, 1)

            def normalise(n, j, source, result, tiles=range(T)):
                act.wait_ge(scale_done[n], 2 * j + 2)
                for t in tiles:
                    nc.scalar.activation(result[:, t], source[:, t], ACT.Identity, bias=nmr[n][:, t:t + 1],
                                         scale=rstd[n][:, t:t + 1]).then_inc(norm_done[n], 1)

            def norm_src(j, slot):
                if exists(j, 1):
                    act.wait_ge(xTp, 2 * j)
                src_landed(act, j, slot)
                normalise(LN_SRC, j, src_sb[:, slot], xhat)

            def v_tile(i, t):
                act.wait_ge(kv_mm, T * i + t + 1)
                nc.scalar.activation(v_sb[:, t, :, 0:P],
                                     pKV[:, 1 - t % 2, D:2 * D].rearrange("p (c n) -> p c n", c=C),
                                     ACT.Copy).then_inc(v_done, 1)

            def k_exp(i, h):
                act.wait_ge(k1_done, T * i + 2 * h + 2)
                nc.scalar.activation(ek[:, 2 * h:2 * h + 2], k1[:, 2 * h:2 * h + 2], ACT.Exp,
                                     bias=minus1[:]).then_inc(ek_done, 1)

            def kv_part(i):
                if exists(i, 1):
                    act.wait_ge(s_mm, i)
                v_tile(i, 0)
                v_tile(i, 1)
                k_exp(i, 0)
                v_tile(i, 2)
                v_tile(i, 3)
                k_exp(i, 1)

            def q_part(i):
                for m in range(C):
                    if exists(i, 1):
                        act.wait_ge(qf_done, 2 * i)
                    act.wait_ge(q_mm, 2 * i + m + 1)
                    nc.scalar.activation(eq[:, m], pQ[:, m], ACT.Relu, bias=bq_neg[:, m:m + 1],
                                         scale=-1.0).then_inc(rq_done, 1)
                    act.wait_ge(rq_done, 2 * i + m + 1)
                    nc.scalar.activation(eq[:, m], eq[:, m], ACT.Exp, scale=-1.0).then_inc(eq_done, 1)

            def attention_step(i, slot):
                norm_src(i + 1, 1 - slot)
                kv_part(i)
                if exists(i, 1):
                    split(i - 1, yTp, yh_done, yT)
                q_part(i)
                split(i + 1, xTp, xh_done, xT)

            def abs_sums(n, raw, half):
                for k in range(4 * half, 4 * half + 4):
                    if n or k:
                        act.wait_ge(abs_done, 8 * n + k)
                    nc.scalar.activation(below[:, 0:D], raw[:].rearrange("p a b -> p (a b)")[:, k * D:(k + 1) * D],
                                         ACT.Abs, accum_out=abs_sum[:, n, k:k + 1]).then_inc(abs_done, 1)

            act.wait_ge(setup_act, 3)
            nc.scalar.activation(warm[:], minus1[:], ACT.Exp)
            norm_src(0, 0)
            split(0, xTp, xh_done, xT)
            kv_part(0)
            norm_src(1, 1)
            act.wait_ge(bq_done, 2 * C)
            q_part(0)
            split(1, xTp, xh_done, xT)
            act.wait_ge(s_wffn, 32)
            abs_sums(0, f1_raw, 0)
            attention_step(1, 1)
            act.wait_ge(w1_scaled, C)
            nc.scalar.activation(w1s[0][:].rearrange("p a b -> p (a b)"), w_scaled[:], ACT.Copy).then_inc(w_hi, 1)
            attention_step(2, 0)
            act.wait_ge(s_wmlp, 32)
            nc.scalar.activation(w2s[0][:], w2_raw[:], ACT.Copy).then_inc(w_hi, 1)
            attention_step(3, 1)
            abs_sums(0, f1_raw, 1)
            attention_step(4, 0)
            abs_sums(1, f2_raw, 0)
            with act.Fori(FIRST, LAST, 2) as i:
                attention_step(i, 1)
                attention_step(i + 1, 0)
            abs_sums(1, f2_raw, 1)
            for i in range(LAST, S - 1):
                attention_step(i, i % 2)
            act.wait_ge(s_x, 16)
            normalise(LN_X, 0, x_in, x1)
            kv_part(S - 1)
            split(S - 2, yTp, yh_done, yT)
            q_part(S - 1)
            split(0, x1Tp, x1h_done, x1T)

            def gelu(j, m):
                if m >= 3:
                    act.wait_ge(hl_done, M * j + m - 2)
                elif exists(j, 1):
                    act.wait_ge(hl_done, M * j)
                act.wait_ge(h_mm, M * j + m + 1)
                nc.scalar.activation(g_sb[:, m % 3], pH[:, m % 4], ACT.Gelu, bias=b1c[:, m:m + 1]).then_inc(g_done, 1)

            def norm_out(i, tiles):
                if exists(i, 2):
                    act.wait_ge(s_out, 16 * (i - 1))
                normalise(LN_Z, i - 1, z_sb, o_sb, tiles)

            def norm_x(j):
                act.wait_ge(x1Tp, 2 * j)
                act.wait_ge(s_x, 16 * (j + 1))
                normalise(LN_X, j, x_in, x1)

            def mlp_step(i, front, ahead):
                if front:
                    for m in range(HEAD):
                        gelu(i + 1, m)
                        if m == 3 and exists(i, 1):
                            norm_out(i, (0, 1))
                        if m == 2 and not exists(i, 1):
                            normalise(LN_R, 0, r2, x2)
                split(i, x2Tp, x2h_done, x2T)
                if front:
                    for m in range(HEAD, M):
                        gelu(i + 1, m)
                    if exists(i, 1):
                        norm_out(i, (2, 3))
                else:
                    norm_out(i, range(T))
                for m in range(M):
                    act.wait_ge(u_mm, M * i + m + 1)
                    if m >= RELU_SLOTS and front:
                        act.wait_ge(ul_done, M * i + m - RELU_SLOTS + 1)
                    elif m >= RELU_SLOTS:
                        act.wait_ge(*last_low(m - RELU_SLOTS))
                    elif exists(i, 1):
                        act.wait_ge(ul_done, M * i)
                    nc.scalar.activation(u_sb[:, m % RELU_SLOTS], pH[:, m % 4], ACT.Relu,
                                         bias=cols[:, COL_FB1 + m:COL_FB1 + m + 1]).then_inc(u_done, 1)
                if ahead:
                    norm_x(i + 2)
                    split(i + 2, x1Tp, x1h_done, x1T)
                if front:
                    act.wait_ge(x2Tp, 2 * (i + 1))
                    act.wait_ge(x2b_done, i + 1)
                    normalise(LN_R, i + 1, r2, x2)

            gelu(0, 0)
            gelu(0, 1)
            split(S - 1, yTp, yh_done, yT)
            for m in range(2, M):
                gelu(0, m)
            norm_x(1)
            split(1, x1Tp, x1h_done, x1T)
            mlp_step(0, True, True)
            with act.Fori(1, S - 2) as i:
                mlp_step(i, True, True)
            mlp_step(S - 2, True, False)
            mlp_step(S - 1, False, False)
            norm_out(S, range(T))

        @block.vector
        def _(dve):
            def stats(n, j, source, tiles=range(T)):
                for t in tiles:
                    nc.vector.bn_stats(bn[n][:, t], source[:, t]).then_inc(stats_done[n], 1)

            def src_stats(j, slot):
                src_landed(dve, j, slot)
                stats(LN_SRC, j, src_sb[:, slot])

            def aggregate(n, j):
                for level in range(4):
                    moments_level(level, dve, n, j)

            def split(j, hi_done, done, parts):
                for c in range(C):
                    dve.wait_ge(hi_done, 2 * j + c + 1)
                    nc.vector.tensor_tensor(parts[1][:, c], pT[:, c], parts[0][:, c].bitcast(F32),
                                            ALU.subtract).then_inc(done, 1)

            def residual(i, slot):
                for h in range(2):
                    dve.wait_ge(o_mm, 2 * i + h + 1)
                    if h == 0:
                        dve.wait_ge(srcb_done, i + 1)
                        if exists(i, 1):
                            dve.wait_ge(s_stored, 16 * i)
                    p = (pS if h == 0 else pA) if isinstance(i, int) and i == S - 1 else pA if h == 0 else pKV[:, 0]
                    nc.vector.tensor_tensor(x_sb[:, 2 * h:2 * h + 2], p.rearrange("p (t d) -> p t d", t=2),
                                            srcb[:, slot, 2 * h:2 * h + 2], ALU.add).then_inc(x_done, 1)

            def k_tile(i, t):
                dve.wait_ge(v_done, T * i + t + 1)
                nc.vector.tensor_tensor(k1[:, t], pKV[:, 1 - t % 2, 0:D], row_k1[:], ALU.add).then_inc(k1_done, 1)

            def k_features(i, h):
                dve.wait_ge(ek_done, 2 * i + h + 1)
                nc.vector.scalar_tensor_tensor(
                    out=kf[:, 2 * h:2 * h + 2], in0=ek[:, 2 * h:2 * h + 2], scalar=1.0,
                    in1=k1[:, 2 * h:2 * h + 2], op0=ALU.min, op1=ALU.max).then_inc(kf_done, 1)

            def q_features(i, m):
                dve.wait_ge(eq_done, 2 * i + m + 1)
                nc.vector.scalar_tensor_tensor(
                    out=qf[:, m], in0=pQ[:, m], scalar=bq_one[:, m:m + 1], in1=eq[:, m],
                    op0=ALU.add, op1=ALU.max).then_inc(qf_done, 1)

            def kv_state(i):
                st = pS[:, 0:C * VW].rearrange("p (c n) -> p c n", c=C)
                dve.wait_ge(s_mm, i + 1)
                nc.vector.tensor_tensor(kvm[:], st[:, :, 0:P],
                                        mask[:, 0:P].rearrange("p (o n) -> p o n", o=1).broadcast_to([P, C, P]),
                                        ALU.mult).then_inc(kvm_done, 1)
                for c in range(C):
                    nc.vector.tensor_scalar(kvz[:, c, P:KW], mask[:, P:KW], st[:, c, P:P + 1], None,
                                            ALU.mult).then_inc(kvz_done, 1)
                dve.wait_ge(kvm_done, i + 1)
                for c in range(C):
                    nc.vector.scalar_tensor_tensor(
                        out=kvz[:, c, 0:P], in0=bv_mask[:, c], scalar=st[:, c, P:P + 1], in1=kvm[:, c],
                        op0=ALU.mult, op1=ALU.add).then_inc(kvz_done, 1)

            def divide(i, h):
                num = (pQ[:] if h == 0 else pT[:]).rearrange("p t (c n) -> p (t c) n", c=C)
                dve.wait_ge(num_mm, 2 * i + h + 1)
                nc.vector.tensor_scalar(den[:, h], num[:, :, P:KW], ATTN_EPS, None, ALU.max).then_inc(den_done, 1)
                dve.wait_ge(den_done, 2 * i + h + 1)
                nc.vector.reciprocal(rden[:, h], den[:, h]).then_inc(rden_done, 1)
                dve.wait_ge(rden_done, 2 * i + h + 1)
                nc.vector.tensor_tensor(
                    y_sb[:, 2 * h:2 * h + 2].rearrange("p t (c h e) -> p (t c) h e", c=C, h=HC),
                    num[:, :, 0:P].rearrange("p a (h e) -> p a h e", h=HC),
                    rden[:, h].rearrange("p a (h o) -> p a h o", o=1).broadcast_to([P, 2 * C, HC, HD]),
                    ALU.mult).then_inc(y_done, 1)

            def attention_step(i, slot, spare1=None, spare2=None, spare3=None):
                last = isinstance(i, int) and i == S - 1
                ahead = not last
                n, j = (LN_X, 0) if isinstance(i, int) and i == S - 2 else (LN_SRC, i + 2)
                k_tile(i, 0)
                k_tile(i, 1)
                if spare1:
                    spare1()
                k_tile(i, 2)
                k_features(i, 0)
                k_tile(i, 3)
                if spare2:
                    spare2()
                k_features(i, 1)
                if exists(i, 1):
                    split(i - 1, yh_done, yl_done, yT)
                if ahead:
                    if n == LN_X:
                        dve.wait_ge(s_x, 16)
                        stats(LN_X, 0, x_in)
                    else:
                        src_stats(j, slot)
                    moments_level(0, dve, n, j)
                q_features(i, 0)
                if ahead:
                    moments_level(1, dve, n, j)
                q_features(i, 1)
                if ahead:
                    moments_level(2, dve, n, j)
                if spare3:
                    spare3()
                kv_state(i)
                if ahead:
                    moments_level(3, dve, n, j)
                    split(i + 1, xh_done, xl_done, xT)
                else:
                    split(0, x1h_done, x1l_done, x1T)
                if exists(i, 1):
                    residual(i - 1, 1 - slot)
                divide(i, 0)
                divide(i, 1)

            def ternary(k):
                n, quarter = k // 4, k % 4
                raw, q = ((f1_raw, fq1), (f2_raw, fq2))[n]
                part = slice(quarter * D * 2, (quarter + 1) * D * 2)
                raw, q = (x[:].rearrange("p a b -> p (a b)")[:, part] for x in (raw, q))
                nc.vector.tensor_scalar(below[:, part], raw, thr_neg[:, n:n + 1], None, ALU.is_lt).then_inc(below_done, 1)
                dve.wait_ge(below_done, k + 1)
                nc.vector.scalar_tensor_tensor(out=q, in0=raw, scalar=thr[:, n:n + 1], in1=below[:, part],
                                               op0=ALU.is_gt, op1=ALU.subtract).then_inc(tern_done, 1)

            def scale_w1(c):
                dve.wait_ge(s_wmlp, 32)
                dve.wait_ge(wsplit, 2 * C + 2)
                nc.vector.tensor_scalar(w_scaled[:, c * F:(c + 1) * F], w1_raw[:, c],
                                        cols[:, COL_G2 + c:COL_G2 + c + 1], None, ALU.mult).then_inc(w1_scaled, 1)

            def shift_b1():
                dve.wait_ge(b1_mm, 1)
                nc.vector.tensor_tensor(b1c[:], pA[:, 0:M], cols[:, COL_B1:COL_B1 + M], ALU.add).then_inc(b1c_done, 1)

            def abs_total():
                dve.wait_ge(abs_done, 16)
                nc.vector.tensor_reduce(abs_tot[:], abs_sum[:], AX.X, ALU.add).then_inc(thr_done, 1)

            def thresholds():
                dve.wait_ge(thr_mm, 1)
                dve.wait_ge(s_mm, LAST + 2)
                nc.vector.tensor_scalar(thr[:], pS[:, THR:THR + 2], 1.0 / (D * F), Q_EPS, ALU.mult,
                                        ALU.add).then_inc(thr_done, 1)
                dve.wait_ge(thr_done, 2)
                nc.vector.tensor_scalar(thr_neg[:], thr[:], -0.5, None, ALU.mult).then_inc(thr_done, 1)
                dve.wait_ge(thr_done, 3)
                nc.vector.tensor_scalar(thr[:], thr[:], 0.5, None, ALU.mult).then_inc(thr_done, 1)
                dve.wait_ge(thr_done, 4)

            dve.memset(ones[:], 1.0).then_inc(setup_dve, 1)
            src_stats(0, 0)
            aggregate(LN_SRC, 0)
            dve.wait_ge(s_vec, 16)
            dve.wait_ge(setup_dve, 1)
            for c in range(C):
                nc.vector.tensor_scalar(be1_wide[:, c], ones[:], cols[:, COL_BE1 + c:COL_BE1 + c + 1], None,
                                        ALU.mult).then_inc(setup_dve, 1)
            dve.wait_ge(s_wqkv, 16)
            qkv_g = w_scaled[:, 0:C * 3 * D].rearrange("p (c n) -> p c n", c=C)
            for c in range(C):
                nc.vector.tensor_scalar(qkv_g[:, c], qkv_raw[:, c], cols[:, COL_G1 + c:COL_G1 + c + 1], None,
                                        ALU.mult).then_inc(scaled, 1)
            dve.wait_ge(scaled, C)
            for c in range(C):
                nc.vector.tensor_copy(wqkv[0][:, c], qkv_g[:, c]).then_inc(wsplit, 1)
            for c in range(C):
                dve.wait_ge(wsplit, c + 1)
                nc.vector.tensor_tensor(wqkv[1][:, c], qkv_g[:, c], wqkv[0][:, c].bitcast(F32),
                                        ALU.subtract).then_inc(wsplit, 1)
            src_stats(1, 1)
            split(0, xh_done, xl_done, xT)
            aggregate(LN_SRC, 1)
            dve.wait_ge(setup_pe_mm, 2)
            dve.wait_ge(s_rows_kv, 16)
            nc.vector.scalar_tensor_tensor(out=row_k1[:], in0=pA[:, 0:D], scalar=1.0, in1=rows_kv[:, 0:D],
                                           op0=ALU.add, op1=ALU.add).then_inc(brow_done, 1)
            dve.wait_ge(s_wout, 16)
            nc.vector.tensor_copy(wout[0][:], out_raw[:]).then_inc(wsplit, 1)
            dve.wait_ge(wsplit, 2 * C + 1)
            nc.vector.tensor_tensor(wout[1][:], out_raw[:], wout[0][:].bitcast(F32),
                                    ALU.subtract).then_inc(wsplit, 1)
            dve.wait_ge(brow_done, 1)

            def more_biases():
                nc.vector.tensor_tensor(row_v[:], pA[:, D:2 * D], rows_kv[:, D:2 * D], ALU.add).then_inc(brow_done, 1)
                for m in range(C):
                    b = cols[:, COL_BQ + m:COL_BQ + m + 1]
                    nc.vector.tensor_scalar(bq_neg[:, m:m + 1], pS[:, m:m + 1], b, -1.0, ALU.add,
                                            ALU.mult).then_inc(bq_done, 1)
                    nc.vector.tensor_scalar(bq_one[:, m:m + 1], pS[:, m:m + 1], b, 1.0, ALU.add,
                                            ALU.add).then_inc(bq_done, 1)

            def v_bias():
                dve.wait_ge(bq_done, 2 * C)
                dve.wait_ge(s_mask, 16)
                dve.wait_ge(brow_done, 2)
                nc.vector.tensor_tensor(bv_mask[:], row_v[:].rearrange("p (c n) -> p c n", c=C),
                                        mask[:, 0:P].rearrange("p (o n) -> p o n", o=1).broadcast_to([P, C, P]),
                                        ALU.mult).then_inc(brow_done, 1)
                dve.wait_ge(brow_done, 3)

            attention_step(0, 0, more_biases, None, v_bias)
            attention_step(1, 1, lambda: scale_w1(0), lambda: (scale_w1(1), shift_b1()))
            for i in range(2, FIRST):
                attention_step(i, i % 2)
            with dve.Fori(FIRST, LAST, 2) as i:
                attention_step(i, 1)
                attention_step(i + 1, 0)
            attention_step(LAST, 1, None, abs_total)
            attention_step(LAST + 1, 0, None, None, thresholds)
            attention_step(LAST + 2, 1, lambda: ternary(0), lambda: ternary(1))
            attention_step(LAST + 3, 0, lambda: (ternary(2), ternary(3)), lambda: ternary(4))
            attention_step(LAST + 4, 1, lambda: ternary(5), lambda: (ternary(6), ternary(7)))

            def split_gelu(j, m):
                dve.wait_ge(g_done, M * j + m + 1)
                nc.vector.tensor_copy(hT[0][:, m], g_sb[:, m % 3]).then_inc(hh_done, 1)
                dve.wait_ge(hh_done, M * j + m + 1)
                nc.vector.tensor_tensor(hT[1][:, m], g_sb[:, m % 3], hT[0][:, m].bitcast(F32),
                                        ALU.subtract).then_inc(hl_done, 1)

            def x_stats(j):
                dve.wait_ge(s_x, 16 * (j + 1))
                stats(LN_X, j, x_in)
                aggregate(LN_X, j)

            def mlp_output(j, ahead):
                for h in range(2):
                    if h == 0:
                        dve.wait_ge(r_done, 2 * (j + 1))
                        if exists(j, 1):
                            dve.wait_ge(x2_done, T * j)
                    dve.wait_ge(w2_mm, 2 * j + h + 1)
                    nc.vector.tensor_tensor(r2[:, 2 * h:2 * h + 2], pO[:, h].rearrange("p (t d) -> p t d", t=2),
                                            r_sb[:, 2 * h:2 * h + 2], ALU.add).then_inc(r2_done, 1)
                    dve.wait_ge(r2_done, 2 * j + h + 1)
                    stats(LN_R, j, r2, (2 * h, 2 * h + 1))
                    if h == 0 and ahead:
                        split(j + 1, x1h_done, x1l_done, x1T)
                aggregate(LN_R, j)

            def mlp_step(i, front, ahead):
                if front:
                    for m in range(HEAD):
                        split_gelu(i + 1, m)
                split(i, x2h_done, x2l_done, x2T)
                if front:
                    for m in range(HEAD, M):
                        split_gelu(i + 1, m)
                if ahead:
                    x_stats(i + 2)
                for m in range(M):
                    dve.wait_ge(u_done, M * i + m + 1)
                    nc.vector.tensor_copy(uT[0][:, m], u_sb[:, m % RELU_SLOTS]).then_inc(uh_done, 1)
                    if not front and m % 2:
                        dve.wait_ge(uh_done, M * i + m + 1)
                        nc.vector.tensor_tensor(uT[1][:, m], u_sb[:, m % RELU_SLOTS], uT[0][:, m].bitcast(F32),
                                                ALU.subtract).then_inc(ul_odd, 1)
                if front:
                    mlp_output(i + 1, ahead)
                for h in range(2):
                    if h == 0:
                        dve.wait_ge(x2b_done, i + 1)
                        if exists(i, 1):
                            dve.wait_ge(out_done, T * i)
                    dve.wait_ge(f_mm, 2 * i + h + 1)
                    nc.vector.tensor_tensor(z_sb[:, 2 * h:2 * h + 2],
                                            pO[:, h].rearrange("p (t d) -> p t d", t=2),
                                            x2b[:, 2 * h:2 * h + 2], ALU.add).then_inc(z_done, 1)
                    dve.wait_ge(z_done, 2 * i + h + 1)
                    stats(LN_Z, i, z_sb, (2 * h, 2 * h + 1))
                aggregate(LN_Z, i)

            split_gelu(0, 0)
            split_gelu(0, 1)
            split(S - 1, yh_done, yl_done, yT)
            split_gelu(0, 2)
            for m in range(3, M):
                split_gelu(0, m)
            residual(S - 1, 1)
            x_stats(1)
            mlp_output(0, True)
            mlp_step(0, True, True)
            with dve.Fori(1, S - 2) as i:
                mlp_step(i, True, True)
            mlp_step(S - 2, True, False)
            mlp_step(S - 1, False, False)

        @block.tensor
        def _(pe):
            def transposes(src_tile, ready):
                for c in range(C):
                    for t in range(T):
                        mm = nc.tensor.transpose(pT[:, c, t * P:(t + 1) * P], src_tile[:, t, c * P:(c + 1) * P],
                                                 ident[:])
                    mm.then_inc(ready, 1)

            def split_product(out_ap, lhs, rhs, chunks):
                for n, (a, w) in enumerate(passes3):
                    for c in range(chunks):
                        mm = nc.tensor.matmul(out_ap, lhs(a, w, c), rhs(a, w, c), start=n == 0 and c == 0,
                                              stop=n == 2 and c == chunks - 1)
                return mm

            def out_projection(i, pair0, pair1, ready):
                for t in range(T):
                    o = (pair0 if t < 2 else pair1)[:, t % 2 * D:(t % 2 + 1) * D]
                    mm = split_product(o, lambda a, w, c: yT[a][:, c, t * P:(t + 1) * P],
                                       lambda a, w, c: wout[w][:, c], C)
                    if t % 2:
                        mm.then_inc(ready, 1)

            def attention_step(i, before_state=None, before_out=None, before_num=None):
                pe.wait_ge(xh_done, 2 * i + 2)
                pe.wait_ge(xl_done, 2 * i + 2)
                for t in range(T):
                    if t == 1 and exists(i, 2):
                        pe.wait_ge(x_done, 2 * (i - 1))
                    if t >= 2:
                        pe.wait_ge(k1_done, T * i + t - 1)
                        pe.wait_ge(v_done, T * i + t - 1)
                    split_product(pKV[:, 1 - t % 2], lambda a, w, c: xT[a][:, c, t * P:(t + 1) * P],
                                  lambda a, w, c: wqkv[w][:, c, D:3 * D], C).then_inc(kv_mm, 1)
                if exists(i, 1):
                    pe.wait_ge(y_done, 2 * i)
                    transposes(y_sb, yTp)
                for m in range(C):
                    split_product(pQ[:, m], lambda a, w, c: wqkv[w][:, c, m * P:(m + 1) * P],
                                  lambda a, w, c: xT[a][:, c], C).then_inc(q_mm, 1)
                pe.wait_ge(kf_done, 2 * i + 2)
                pe.wait_ge(v_done, T * i + T)
                if before_state:
                    before_state()
                for c in range(C):
                    for t in range(T):
                        mm = nc.tensor.matmul(pS[:, c * VW:(c + 1) * VW], kf[:, t, c * P:(c + 1) * P],
                                              v_sb[:, t, c], start=t == 0, stop=t == T - 1)
                mm.then_inc(s_mm, 1)
                if exists(i, 1):
                    pe.wait_ge(yh_done, 2 * i)
                    pe.wait_ge(yl_done, 2 * i)
                if isinstance(i, int) and i == S - 1:
                    pe.wait_ge(x1_done, T)
                    transposes(x1, x1Tp)
                else:
                    pe.wait_ge(xhat_done, T * (i + 1) + T)
                    transposes(xhat, xTp)
                if before_out:
                    before_out()
                if exists(i, 1):
                    out_projection(i - 1, pA, pKV[:, 0], o_mm)
                if before_num:
                    before_num()
                pe.wait_ge(kvz_done, 2 * C * (i + 1))
                pe.wait_ge(qf_done, 2 * i + 2)
                for t in range(T):
                    if t == 2:
                        if isinstance(i, int) and i == S - 1:
                            pe.wait_ge(x1l_done, 2)
                        else:
                            pe.wait_ge(xl_done, 2 * (i + 2))
                    for c in range(C):
                        mm = nc.tensor.matmul((pQ if t < 2 else pT)[:, t % 2, c * D:c * D + KW],
                                              qf[:, c, t * P:(t + 1) * P], kvz[:, c], start=True, stop=True)
                    if t % 2:
                        mm.then_inc(num_mm, 1)

            pe.wait_ge(s_vec, 16)
            pe.wait_ge(s_wqkv, 16)
            for m in range(C):
                for c in range(C):
                    mm = nc.tensor.matmul(pS[:, m:m + 1], qkv_raw[:, c, m * P:(m + 1) * P],
                                          cols[:, COL_BE1 + c:COL_BE1 + c + 1], start=c == 0, stop=c == C - 1)
            mm.then_inc(setup_pe_mm, 1)
            pe.wait_ge(setup_dve, 1 + C)

            def shift_kv(c):
                return nc.tensor.matmul(pA, be1_wide[:, c], qkv_raw[:, c, D:3 * D], start=c == 0, stop=c == C - 1)

            shift_kv(0)
            pe.wait_ge(s_const, 16)
            pe.wait_ge(xhat_done, T)
            transposes(xhat, xTp)
            shift_kv(1).then_inc(setup_pe_mm, 1)
            pe.wait_ge(wsplit, 2 * C)

            def shift_w1():
                pe.wait_ge(brow_done, 2)
                pe.wait_ge(s_wmlp, 32)
                for m in range(M):
                    for c in range(C):
                        mm = nc.tensor.matmul(pA[:, m:m + 1], w1_raw[:, c, m * P:(m + 1) * P],
                                              cols[:, COL_BE2 + c:COL_BE2 + c + 1], start=c == 0, stop=c == C - 1)
                mm.then_inc(b1_mm, 1)

            def abs_over_partitions():
                pe.wait_ge(thr_done, 1)
                nc.tensor.matmul(pS[:, THR:THR + 2], ones[:], abs_tot[:], start=True, stop=True).then_inc(thr_mm, 1)

            attention_step(0, before_num=shift_w1)
            pe.wait_ge(wsplit, 2 * C + 2)
            attention_step(1, before_out=lambda: pe.wait_ge(b1c_done, 1))
            for i in range(2, FIRST):
                attention_step(i)
            with pe.Fori(FIRST, LAST) as i:
                attention_step(i)
            attention_step(LAST)
            attention_step(LAST + 1, before_state=abs_over_partitions)
            attention_step(LAST + 2, before_state=lambda: pe.wait_ge(thr_done, 2))
            for i in range(LAST + 3, S):
                attention_step(i)

            def mlp_up(j, m):
                if m >= 4:
                    pe.wait_ge(g_done, M * j + m - 3)
                split_product(pH[:, m % 4], lambda a, w, c: w1s[w][:, c, m * P:(m + 1) * P],
                              lambda a, w, c: x1T[a][:, c], C).then_inc(h_mm, 1)

            def mlp_down(j, ahead):
                pe.wait_ge(hh_done, M * (j + 1))
                pe.wait_ge(hl_done, M * (j + 1))
                for t in range(T):
                    if t == 2 and ahead:
                        pe.wait_ge(x1_done, T * (j + 2))
                        transposes(x1, x1Tp)
                    if t % 2 == 0 and exists(j, 2):
                        pe.wait_ge(z_done, 2 * (j - 2) + t // 2 + 1)
                    elif t % 2 == 0 and isinstance(j, int) and j == 0:
                        pe.wait_ge(x_done, 2 * (S - 1) + t // 2 + 1)
                    mm = split_product(pO[:, t // 2, t % 2 * D:(t % 2 + 1) * D],
                                       lambda a, w, m: hT[a][:, m, t * P:(t + 1) * P],
                                       lambda a, w, m: w2s[w][:, m], M)
                    if t % 2:
                        mm.then_inc(w2_mm, 1)

            def ffn_up(i, front):
                pe.wait_ge(x2h_done, 2 * (i + 1))
                pe.wait_ge(x2l_done, 2 * (i + 1))
                for m in range(M):
                    if m < 4 and front:
                        pe.wait_ge(g_done, M * (i + 1) + m + 5)
                    if m >= 4:
                        pe.wait_ge(u_done, M * i + m - 3)
                    for a in range(2):
                        for c in range(C):
                            mm = nc.tensor.matmul(pH[:, m % 4], fq1[:, c, m * P:(m + 1) * P], x2T[a][:, c],
                                                  start=a == 0 and c == 0, stop=a == 1 and c == C - 1)
                    mm.then_inc(u_mm, 1)

            def ffn_down(i, front):
                pe.wait_ge(uh_done, M * (i + 1))
                if front:
                    pe.wait_ge(ul_done, M * (i + 1))
                else:
                    pe.wait_ge(*last_low(M - 2))
                    pe.wait_ge(*last_low(M - 1))
                for t in range(T):
                    if t % 2 == 0 and front:
                        pe.wait_ge(r2_done, 2 * (i + 1) + t // 2 + 1)
                    elif t % 2 == 0:
                        pe.wait_ge(z_done, 2 * (i - 1) + t // 2 + 1)
                    for a in range(2):
                        for m in range(M):
                            mm = nc.tensor.matmul(pO[:, t // 2, t % 2 * D:(t % 2 + 1) * D],
                                                  uT[a][:, m, t * P:(t + 1) * P], fq2[:, m],
                                                  start=a == 0 and m == 0, stop=a == 1 and m == M - 1)
                    if t % 2:
                        mm.then_inc(f_mm, 1)

            def mlp_step(i, front, ahead):
                if front:
                    pe.wait_ge(x1h_done, 2 * (i + 2))
                    pe.wait_ge(x1l_done, 2 * (i + 2))
                    for m in range(HEAD):
                        mlp_up(i + 1, m)
                pe.wait_ge(x2_done, T * (i + 1))
                transposes(x2, x2Tp)
                if front:
                    for m in range(HEAD, M):
                        mlp_up(i + 1, m)
                ffn_up(i, front)
                if front:
                    mlp_down(i + 1, ahead)
                ffn_down(i, front)

            pe.wait_ge(x1h_done, 2)
            pe.wait_ge(x1l_done, 2)
            pe.wait_ge(b1c_done, 1)
            pe.wait_ge(tern_done, 8)
            pe.wait_ge(w_lo, 2)
            pe.wait_ge(x_done, 2 * (S - 1))
            pe.wait_ge(k1_done, T * S)
            mlp_up(0, 0)
            mlp_up(0, 1)
            pe.wait_ge(y_done, 2 * S)
            transposes(y_sb, yTp)
            for m in range(2, M):
                mlp_up(0, m)
            pe.wait_ge(yh_done, 2 * S)
            pe.wait_ge(yl_done, 2 * S)
            out_projection(S - 1, pS, pA, o_mm)
            mlp_down(0, True)
            mlp_step(0, True, True)
            with pe.Fori(1, S - 2) as i:
                mlp_step(i, True, True)
            mlp_step(S - 2, True, False)
            mlp_step(S - 1, False, False)


def kernel(L0_attn_src, L0_attn_qkv_w, L0_attn_qkv_b, L0_attn_out_w, L0_attn_out_b, L0_attn_w1, L0_attn_b1,
           L0_attn_w2, L0_attn_b2, L0_attn_g1, L0_attn_be1, L0_attn_g2, L0_attn_be2, L0_ffn_W1, L0_ffn_b1,
           L0_ffn_W2, L0_ffn_b2):
    import numpy as np
    import concourse.bacc as bacc
    from concourse.bass_utils import run_bass_kernel_spmd

    def column(v):
        return np.asarray(v).reshape(-1, P).T

    qkv_b = np.asarray(L0_attn_qkv_b)
    cols = np.concatenate([column(v) for v in (L0_attn_g1, L0_attn_be1, L0_attn_g2, L0_attn_be2, qkv_b[:D],
                                               L0_attn_b1, L0_ffn_b1)], axis=1)
    rows = np.concatenate([qkv_b[D:], np.asarray(L0_attn_out_b), np.asarray(L0_attn_b2), np.asarray(L0_ffn_b2)])
    head = np.arange(P) // HD
    const = np.concatenate([np.eye(P), head[:, None] == head[None, :], head[:, None] == np.arange(HC)[None, :]],
                           axis=1).astype(np.float32)
    arrays = {
        "src": L0_attn_src, "qkv_w": L0_attn_qkv_w, "out_w": L0_attn_out_w, "w1": L0_attn_w1, "w2": L0_attn_w2,
        "fw1": np.asarray(L0_ffn_W1).T, "fw2": np.asarray(L0_ffn_W2).T, "cols": cols, "rows": rows[None, :],
        "const": const,
    }
    arrays = {name: np.ascontiguousarray(a) for name, a in arrays.items()}
    nc = bacc.Bacc("TRN2", target_bir_lowering=False, num_devices=1)
    args = [nc.dram_tensor(name + "_dram", a.shape, mybir.dt.from_np(a.dtype), kind="ExternalInput").ap()
            for name, a in arrays.items()]
    out = nc.dram_tensor("out_dram", (S, N, D), F32, kind="ExternalOutput").ap()
    build(nc, *args, out)
    r = run_bass_kernel_spmd(nc, [{name + "_dram": a for name, a in arrays.items()}], core_ids=[0])
    return r.results[0]["out_dram"]
```

```python
from contextlib import ExitStack

import concourse.bass as bass
from concourse import mybir

P = 128
D = 256
F = 1024
S = 16
N = 512
T = N // P
C = D // P
M = F // P
HEADS = 16
HD = D // HEADS
HC = P // HD
VW = P + 2
KW = P + HC
LN_EPS = 1e-5
ATTN_EPS = 1e-6
Q_EPS = 1e-5

F32 = mybir.dt.float32
F32R = mybir.dt.float32r
ALU = mybir.AluOpType
ACT = mybir.ActivationFunctionType
AX = mybir.AxisListType

COL_G1, COL_BE1, COL_G2, COL_BE2, COL_BQ, COL_B1 = (n * C for n in range(6))
COL_FB1 = COL_B1 + M
COLS = COL_FB1 + M
ROW_KV, ROW_OUT, ROW_B2, ROW_FB2 = (n * D for n in (0, 2, 3, 4))
LN_SRC, LN_X, LN_R, LN_Z = range(4)


def exists(i, back):
    return not isinstance(i, int) or i >= back


def build(nc, src, qkv_w, out_w, w1, w2, fw1, fw2, cols_in, rows_in, const_in, out):
    src_rows = src.rearrange("s (p t) d -> (s p) (t d)", t=T)
    out_rows = out.rearrange("s (p t) d -> (s p) (t d)", t=T)
    x_dram = nc.dram_tensor("x_dram", (S * P, T * D), F32, kind="Internal").ap()

    with ExitStack() as whole:
        def sb(stack, name, shape, dt=F32):
            return stack.enter_context(nc.sbuf_tensor(name, shape, dt))

        def sem(*names):
            return [whole.enter_context(nc.semaphore(n)) for n in names]

        wqkv = [sb(whole, f"wqkv_{k}", [P, C, 3 * D], F32R) for k in "hl"]
        wout = [sb(whole, f"wout_{k}", [P, C, D], F32R) for k in "hl"]
        w1s = [sb(whole, f"w1_{k}", [P, C, F], F32R) for k in "hl"]
        w2s = [sb(whole, f"w2_{k}", [P, M, D], F32R) for k in "hl"]
        fq1 = sb(whole, "fq1", [P, C, F], F32R)
        fq2 = sb(whole, "fq2", [P, M, D], F32R)
        cols = sb(whole, "cols", [P, COLS])
        ident = sb(whole, "ident", [P, P])
        b1c = sb(whole, "b1c", [P, M])
        row_b2 = sb(whole, "row_b2", [P, D])
        row_fb2 = sb(whole, "row_fb2", [P, D])
        half4 = sb(whole, "half4", [P, T])
        minus1 = sb(whole, "minus1", [P, 1])
        warm = sb(whole, "warm", [P, 1])
        bn = [sb(whole, f"bn{n}", [P, T, 6]) for n in range(4)]
        moments = [(sb(whole, f"pair{n}", [P, T, 2]), sb(whole, f"dif{n}", [P, T]), sb(whole, f"var{n}", [P, T]))
                   for n in range(4)]
        veps = [sb(whole, f"veps{n}", [P, T]) for n in range(4)]
        nmean = [sb(whole, f"nmean{n}", [P, T]) for n in range(4)]
        rstd = [sb(whole, f"rstd{n}", [P, T]) for n in range(4)]
        nmr = [sb(whole, f"nmr{n}", [P, T]) for n in range(4)]

        with ExitStack() as ph:
            qkv_raw = sb(ph, "qkv_raw", [P, C, 3 * D])
            out_raw = sb(ph, "out_raw", [P, C, D])
            w1_raw = sb(ph, "w1_raw", [P, C, F])
            w2_raw = sb(ph, "w2_raw", [P, M, D])
            w_scaled = sb(ph, "w_scaled", [P, C * F])
            below = sb(ph, "below", [P, C * F])
            f1_raw = sb(ph, "f1_raw", [P, C, F])
            f2_raw = sb(ph, "f2_raw", [P, M, D])
            rows_kv = sb(ph, "rows_kv", [P, 2 * D])
            row_v = sb(ph, "row_v", [P, D])
            be1_wide = sb(ph, "be1_wide", [P, C, P])
            mask = sb(ph, "mask", [P, KW])
            ones = sb(ph, "ones", [P, P])
            row_k1 = sb(ph, "row_k1", [P, D])
            row_out = sb(ph, "row_out", [P, D])
            bv_mask = sb(ph, "bv_mask", [P, C, P])
            bq_neg = sb(ph, "bq_neg", [P, C])
            bq_one = sb(ph, "bq_one", [P, C])
            abs_sum = sb(ph, "abs_sum", [P, 2, 8])
            abs_tot = sb(ph, "abs_tot", [P, 2])
            thr = sb(ph, "thr", [P, 2])
            thr_neg = sb(ph, "thr_neg", [P, 2])

            src_sb = sb(ph, "src_sb", [P, 2, T, D])
            srcb = sb(ph, "srcb", [P, 2, T, D])
            xhat = sb(ph, "xhat", [P, T, D])
            xT = [sb(ph, f"xT_{k}", [P, C, N], F32R) for k in "hl"]
            k1 = sb(ph, "k1", [P, T, D])
            ek = sb(ph, "ek", [P, T, D])
            kf = sb(ph, "kf", [P, T, D])
            v_sb = sb(ph, "v_sb", [P, T, C, VW])
            eq = sb(ph, "eq", [P, C, N])
            qf = sb(ph, "qf", [P, C, N])
            kvm = sb(ph, "kvm", [P, C, P])
            kvz = sb(ph, "kvz", [P, C, KW])
            den = sb(ph, "den", [P, 2, 2 * C, HC])
            rden = sb(ph, "rden", [P, 2, 2 * C, HC])
            y_sb = sb(ph, "y_sb", [P, T, D])
            yT = [sb(ph, f"yT_{k}", [P, C, N], F32R) for k in "hl"]
            x_sb = sb(ph, "x_sb", [P, T, D])

        with ExitStack() as ph:
            x_in = sb(ph, "x_in", [P, T, D])
            r_sb = sb(ph, "r_sb", [P, T, D])
            x1 = sb(ph, "x1", [P, T, D])
            x1T = [sb(ph, f"x1T_{k}", [P, C, N], F32R) for k in "hl"]
            g_sb = sb(ph, "g_sb", [P, 3, N])
            hT = [sb(ph, f"hT_{k}", [P, M, N], F32R) for k in "hl"]
            z_sb = sb(ph, "z_sb", [P, T, D])
            u_sb = sb(ph, "u_sb", [P, M, N])
            uT = [sb(ph, f"uT_{k}", [P, M, N], F32R) for k in "hl"]
            r2 = sb(ph, "r2", [P, T, D])
            x2 = sb(ph, "x2", [P, T, D])
            x2b = sb(ph, "x2b", [P, T, D])
            x2T = [sb(ph, f"x2T_{k}", [P, C, N], F32R) for k in "hl"]
            o_sb = sb(ph, "o_sb", [P, T, D])

        pT = whole.enter_context(nc.psum_tensor("pT", [P, C, N], F32))
        pH = whole.enter_context(nc.psum_tensor("pH", [P, 4, N], F32))
        pO = whole.enter_context(nc.psum_tensor("pO", [P, 2, N], F32))
        pKV = pH[:, 0:2]
        pQ = pH[:, 2:4]
        pS = pO[:, 0]
        pA = pO[:, 1]

        (s_vec, s_wqkv, s_wout, s_w1, s_w2, s_f1, s_f2, s_const, s_src0, s_src1, s_stored, s_x, s_res, s_out) = sem(
            "s_vec", "s_wqkv", "s_wout", "s_w1", "s_w2", "s_f1", "s_f2", "s_const", "s_src0", "s_src1", "s_stored",
            "s_x", "s_res", "s_out")
        s_rows, s_rows_kv, s_rows_out, s_mask = sem("s_rows", "s_rows_kv", "s_rows_out", "s_mask")
        s_src = [s_src0, s_src1]
        (setup_dve, setup_act, setup_pe_mm, b1_mm, thr_mm, scaled, wsplit, w1_scaled, w_hi, w_lo, brow_done,
         bq_done, b1c_done, abs_done, thr_done, below_done, tern_done) = sem(
            "setup_dve", "setup_act", "setup_pe_mm", "b1_mm", "thr_mm", "scaled", "wsplit", "w1_scaled", "w_hi",
            "w_lo", "brow_done", "bq_done", "b1c_done", "abs_done", "thr_done", "below_done", "tern_done")
        stats_done = sem("stats0", "stats1", "stats2", "stats3")
        levels = sem("levels0", "levels1", "levels2", "levels3")
        moments_done = sem("moments0", "moments1", "moments2", "moments3")
        scale_done = sem("scale0", "scale1", "scale2", "scale3")
        norm_done = sem("xhat_done", "x1_done", "x2_done", "out_done")
        xhat_done, x1_done, x2_done, out_done = norm_done
        (srcb_done, xTp, xh_done, xl_done, kv_mm, k1_done, v_done, ek_done, kf_done, q_mm, rq_done, eq_done,
         qf_done, s_mm, kvm_done, kvz_done, num_mm, den_done, rden_done, y_done, yTp, yh_done, yl_done, o_mm,
         x_done) = sem(
            "srcb_done", "xTp", "xh_done", "xl_done", "kv_mm", "k1_done", "v_done", "ek_done", "kf_done", "q_mm",
            "rq_done", "eq_done", "qf_done", "s_mm", "kvm_done", "kvz_done", "num_mm", "den_done", "rden_done",
            "y_done", "yTp", "yh_done", "yl_done", "o_mm", "x_done")
        (x1Tp, x1h_done, x1l_done, h_mm, g_done, hh_done, hl_done, r_done, w2_mm, r2_done, x2Tp, x2h_done,
         x2l_done, u_mm, u_done, uh_done, ul_done, ul_odd, x2b_done, f_mm, z_done,
         last_mm, last_z, last_levels, last_moments_done, last_scaled, last_even, last_odd) = sem(
            "x1Tp", "x1h_done", "x1l_done", "h_mm", "g_done", "hh_done", "hl_done", "r_done", "w2_mm", "r2_done",
            "x2Tp", "x2h_done", "x2l_done", "u_mm", "u_done", "uh_done", "ul_done", "ul_odd", "x2b_done", "f_mm",
            "z_done",
            "last_mm", "last_z", "last_levels", "last_moments_done", "last_scaled", "last_even", "last_odd")

        passes3 = [(0, 0), (0, 1), (1, 0)]
        FIRST, LAST = 5, 11
        SIDE = 2 * VW + 40
        HEAD = 6

        def last_bank(t):
            return pO[:, t, 0:D] if t < 2 else pT[:, t - 2, 0:D]

        def last_low(m):
            return (ul_odd, m // 2 + 1) if m % 2 else (ul_done, M * (S - 1) + m // 2 + 1)

        def rows_of(dram, j):
            return dram[j * P:(j + 1) * P, :] if isinstance(j, int) else dram[bass.ds(j * P, P), :]

        def moments_level(level, dve, n, j):
            pair, dif, var = moments[n]
            if level == 0:
                dve.wait_ge(stats_done[n], T * j + T)
                nc.vector.tensor_tensor(pair[:], bn[n][:, :, 1:3], bn[n][:, :, 4:6], ALU.add).then_inc(levels[n], 1)
                nc.vector.tensor_tensor(dif[:], bn[n][:, :, 1], bn[n][:, :, 4], ALU.subtract).then_inc(levels[n], 1)
            if level == 1:
                if exists(j, 1):
                    dve.wait_ge(scale_done[n], 2 * j)
                dve.wait_ge(levels[n], 4 * j + 1)
                nc.vector.tensor_scalar(nmean[n][:], pair[:, :, 0], -0.5, None, ALU.mult).then_inc(moments_done[n], 1)
                dve.wait_ge(levels[n], 4 * j + 2)
                nc.vector.scalar_tensor_tensor(out=dif[:], in0=dif[:], scalar=0.25, in1=dif[:], op0=ALU.mult,
                                               op1=ALU.mult).then_inc(levels[n], 1)
            if level == 2:
                dve.wait_ge(levels[n], 4 * j + 3)
                nc.vector.scalar_tensor_tensor(out=var[:], in0=pair[:, :, 1], scalar=1.0 / D, in1=dif[:],
                                               op0=ALU.mult, op1=ALU.add).then_inc(levels[n], 1)
            if level == 3:
                dve.wait_ge(levels[n], 4 * j + 4)
                nc.vector.tensor_scalar(veps[n][:], var[:], LN_EPS, None, ALU.add).then_inc(moments_done[n], 1)

        def scale(pool, n, j):
            if exists(j, 1):
                pool.wait_ge(norm_done[n], T * j)
            pool.wait_ge(moments_done[n], 2 * j + 2)
            nc.gpsimd.tensor_tensor(rstd[n][:], veps[n][:], half4[:], ALU.pow).then_inc(scale_done[n], 1)
            pool.wait_ge(scale_done[n], 2 * j + 1)
            nc.gpsimd.tensor_tensor(nmr[n][:], nmean[n][:], rstd[n][:], ALU.mult).then_inc(scale_done[n], 1)

        block = whole.enter_context(nc.Block())

        def src_landed(engine, j, slot):
            engine.wait_ge(s_src[slot], 16 * (j // 2 + 1) if isinstance(j, int) else j * 8 + (8 if slot else 16))

        @block.sync
        def _(sp):
            sp.dma_start(src_sb[:, 0], src_rows[0:P, :]).then_inc(s_src[0], 16)
            sp.dma_start(ident[:], const_in[:, 0:P]).then_inc(s_const, 16)
            sp.dma_start(rows_kv[:], rows_in[:, ROW_KV:ROW_KV + 2 * D].broadcast_to([P, 2 * D])).then_inc(s_rows_kv, 16)
            sp.dma_start(src_sb[:, 1], src_rows[P:2 * P, :]).then_inc(s_src[1], 16)
            sp.dma_start(row_out[:], rows_in[:, ROW_OUT:ROW_OUT + D].broadcast_to([P, D])).then_inc(s_rows_out, 16)
            sp.dma_start(mask[:], const_in[:, P:P + KW]).then_inc(s_mask, 16)
            sp.dma_start(out_raw[:], out_w.rearrange("(c p) n -> p c n", p=P)).then_inc(s_wout, 16)
            sp.dma_start(w1_raw[:], w1.rearrange("(c p) n -> p c n", p=P)).then_inc(s_w1, 16)

            def attention_step(i, slot, more):
                if more:
                    sp.wait_ge(srcb_done, i + 1)
                    sp.wait_ge(xhat_done, T * i + T)
                    sp.dma_start(src_sb[:, slot], rows_of(src_rows, i + 2)).then_inc(s_src[slot], 16)
                if exists(i, 1):
                    sp.wait_ge(x_done, 2 * i)
                    sp.dma_start(rows_of(x_dram, i - 1), x_sb[:]).then_inc(s_stored, 16)

            attention_step(0, 0, True)
            sp.dma_start(f1_raw[:], fw1.rearrange("(c p) n -> p c n", p=P)).then_inc(s_f1, 16)
            sp.dma_start(w2_raw[:], w2.rearrange("(m p) n -> p m n", p=P)).then_inc(s_w2, 16)
            sp.dma_start(f2_raw[:], fw2.rearrange("(m p) n -> p m n", p=P)).then_inc(s_f2, 16)
            sp.dma_start(row_b2[:], rows_in[:, ROW_B2:ROW_B2 + D].broadcast_to([P, D])).then_inc(s_rows, 16)
            sp.dma_start(row_fb2[:], rows_in[:, ROW_FB2:ROW_FB2 + D].broadcast_to([P, D])).then_inc(s_rows, 16)
            for i in range(1, FIRST):
                attention_step(i, i % 2, True)
            with sp.Fori(FIRST, LAST, 2) as i:
                attention_step(i, 1, True)
                attention_step(i + 1, 0, True)
            for i in range(LAST, S - 2):
                attention_step(i, i % 2, True)
            sp.wait_ge(s_stored, 16 * (S - 3))
            sp.wait_ge(w_lo, 2)
            sp.dma_start(x_in[:], rows_of(x_dram, 0)).then_inc(s_x, 16)
            sp.dma_start(r_sb[:], rows_of(src_rows, 0)).then_inc(s_res, 16)
            attention_step(S - 2, 0, False)
            attention_step(S - 1, 1, False)

            def load_x(j):
                sp.wait_ge(r_done, 2 * j)
                sp.dma_start(x_in[:], rows_of(x_dram, j)).then_inc(s_x, 16)

            def load_residual(j):
                sp.wait_ge(r2_done, 2 * j)
                sp.dma_start(r_sb[:], rows_of(src_rows, j)).then_inc(s_res, 16)

            def mlp_step(i, ahead):
                if ahead:
                    load_x(i + 2)
                if exists(i, 1):
                    sp.wait_ge(out_done, T * i)
                    sp.dma_start(rows_of(out_rows, i - 1), o_sb[:]).then_inc(s_out, 16)
                if ahead:
                    load_residual(i + 2)

            load_x(1)
            attention_step(S, 0, False)
            load_residual(1)
            sp.wait_ge(s_stored, 16 * S)
            mlp_step(0, True)
            with sp.Fori(1, S - 2) as i:
                mlp_step(i, True)
            mlp_step(S - 2, False)
            mlp_step(S - 1, False)
            for h in range(2):
                sp.wait_ge(last_even, h + 1)
                sp.wait_ge(last_odd, h + 1)
                sp.dma_start(rows_of(out_rows, S - 1)[:, 2 * h * D:2 * (h + 1) * D],
                             o_sb[:, 2 * h:2 * h + 2]).then_inc(s_out, 16)
            sp.wait_ge(s_out, 16 * (S + 1))

        @block.gpsimd
        def _(pool):
            pool.memset(minus1[:], -1.0).then_inc(setup_act, 1)
            pool.memset(half4[:], -0.5).then_inc(setup_act, 1)
            pool.memset(v_sb[:, :, :, P:VW], 1.0).then_inc(setup_act, 1)
            pool.wait_ge(setup_act, 3)

            def add_bias(j, slot):
                if exists(j, 2):
                    pool.wait_ge(x_done, 2 * j - 2)
                src_landed(pool, j, slot)
                for t in range(T):
                    last = nc.gpsimd.tensor_tensor(srcb[:, slot, t], src_sb[:, slot, t], row_out[:], ALU.add)
                last.then_inc(srcb_done, 1)

            def low_part(raw, parts, n):
                pool.wait_ge(w_hi, n + 1)
                nc.gpsimd.tensor_tensor(parts[1][:].rearrange("p a b -> p (a b)"), raw,
                                        parts[0][:].bitcast(F32).rearrange("p a b -> p (a b)"),
                                        ALU.subtract).then_inc(w_lo, 1)

            def attention_step(i, slot):
                scale(pool, LN_SRC, i + 2)
                add_bias(i + 1, 1 - slot)

            scale(pool, LN_SRC, 0)
            pool.wait_ge(s_rows_out, 16)
            add_bias(0, 0)
            scale(pool, LN_SRC, 1)
            for i in range(FIRST):
                attention_step(i, i % 2)
                if i == 2:
                    low_part(w_scaled[:], w1s, 0)
                if i == 3:
                    low_part(w2_raw[:].rearrange("p a b -> p (a b)"), w2s, 1)
            with pool.Fori(FIRST, LAST, 2) as i:
                attention_step(i, 1)
                attention_step(i + 1, 0)
            for i in range(LAST, S - 2):
                attention_step(i, i % 2)
            scale(pool, LN_X, 0)
            add_bias(S - 1, 1)

            def mlp_step(i, back, front, ahead):
                if exists(i, 1):
                    scale(pool, LN_Z, i - 1)
                if front:
                    pool.wait_ge(s_res, 16 * (i + 2))
                    pool.wait_ge(s_x, 16 * (i + 2))
                    nc.gpsimd.tensor_tensor(r_sb[:], r_sb[:], x_in[:], ALU.add).then_inc(r_done, 1)
                    pool.wait_ge(r_done, 2 * (i + 1) + 1)
                    pool.wait_ge(x1_done, T * (i + 2))
                    nc.gpsimd.tensor_tensor(r_sb[:], r_sb[:],
                                            row_b2[:].rearrange("p (o d) -> p o d", o=1).broadcast_to([P, T, D]),
                                            ALU.add).then_inc(r_done, 1)
                if back and front:
                    add_ffn_bias(i)
                if ahead:
                    scale(pool, LN_X, i + 2)
                if back:
                    for m in range(0, M, 1 if front else 2):
                        pool.wait_ge(uh_done, M * i + m + 1)
                        nc.gpsimd.tensor_tensor(uT[1][:, m], u_sb[:, m],
                                                uT[0][:, m].bitcast(F32), ALU.subtract).then_inc(ul_done, 1)
                if front:
                    scale(pool, LN_R, i + 1)
                else:
                    add_ffn_bias(i)

            def add_ffn_bias(i):
                if exists(i, 1):
                    pool.wait_ge(z_done, 2 * i)
                pool.wait_ge(x2_done, T * (i + 1))
                nc.gpsimd.tensor_tensor(x2b[:], x2[:],
                                        row_fb2[:].rearrange("p (o d) -> p o d", o=1).broadcast_to([P, T, D]),
                                        ALU.add).then_inc(x2b_done, 1)

            pool.wait_ge(s_rows, 32)
            mlp_step(-1, False, True, True)
            mlp_step(0, True, True, True)
            with pool.Fori(1, S - 2) as i:
                mlp_step(i, True, True, True)
            mlp_step(S - 2, True, True, False)
            mlp_step(S - 1, True, False, False)
            pool.wait_ge(out_done, T * (S - 1))
            for h in range(2):
                pool.wait_ge(last_moments_done, 2 * h + 2)
                part = slice(2 * h, 2 * h + 2)
                nc.gpsimd.tensor_tensor(rstd[LN_Z][:, part], veps[LN_Z][:, part], half4[:, part],
                                        ALU.pow).then_inc(last_scaled, 1)
                pool.wait_ge(last_scaled, 2 * h + 1)
                nc.gpsimd.tensor_tensor(nmr[LN_Z][:, part], nmean[LN_Z][:, part], rstd[LN_Z][:, part],
                                        ALU.mult).then_inc(last_scaled, 1)

        @block.scalar
        def _(act):
            act.dma_start(cols[:], cols_in).then_inc(s_vec, 16)
            act.dma_start(qkv_raw[:], qkv_w.rearrange("(c p) n -> p c n", p=P)).then_inc(s_wqkv, 16)

            def split(j, ps_ready, done, parts):
                for c in range(C):
                    act.wait_ge(ps_ready, 2 * j + c + 1)
                    nc.scalar.activation(parts[0][:, c], pT[:, c], ACT.Copy).then_inc(done, 1)

            def normalise(n, j, source, result, tiles=range(T)):
                act.wait_ge(scale_done[n], 2 * j + 2)
                for t in tiles:
                    nc.scalar.activation(result[:, t], source[:, t], ACT.Identity, bias=nmr[n][:, t:t + 1],
                                         scale=rstd[n][:, t:t + 1]).then_inc(norm_done[n], 1)

            def norm_src(j, slot):
                if exists(j, 1):
                    act.wait_ge(xTp, 2 * j)
                src_landed(act, j, slot)
                normalise(LN_SRC, j, src_sb[:, slot], xhat)

            def v_tile(i, t):
                act.wait_ge(kv_mm, T * i + t + 1)
                nc.scalar.activation(v_sb[:, t, :, 0:P],
                                     pKV[:, 1 - t % 2, D:2 * D].rearrange("p (c n) -> p c n", c=C),
                                     ACT.Copy).then_inc(v_done, 1)

            def k_exp(i, h):
                act.wait_ge(k1_done, T * i + 2 * h + 2)
                nc.scalar.activation(ek[:, 2 * h:2 * h + 2], k1[:, 2 * h:2 * h + 2], ACT.Exp,
                                     bias=minus1[:]).then_inc(ek_done, 1)

            def kv_part(i):
                if exists(i, 1):
                    act.wait_ge(s_mm, i)
                v_tile(i, 0)
                v_tile(i, 1)
                k_exp(i, 0)
                v_tile(i, 2)
                v_tile(i, 3)
                k_exp(i, 1)

            def q_part(i):
                for m in range(C):
                    if exists(i, 1):
                        act.wait_ge(qf_done, 2 * i)
                    act.wait_ge(q_mm, 2 * i + m + 1)
                    nc.scalar.activation(eq[:, m], pQ[:, m], ACT.Relu, bias=bq_neg[:, m:m + 1],
                                         scale=-1.0).then_inc(rq_done, 1)
                    act.wait_ge(rq_done, 2 * i + m + 1)
                    nc.scalar.activation(eq[:, m], eq[:, m], ACT.Exp, scale=-1.0).then_inc(eq_done, 1)

            def attention_step(i, slot):
                norm_src(i + 1, 1 - slot)
                kv_part(i)
                if exists(i, 1):
                    split(i - 1, yTp, yh_done, yT)
                q_part(i)
                split(i + 1, xTp, xh_done, xT)

            def abs_sums(n, raw, half):
                for k in range(4 * half, 4 * half + 4):
                    if n or k:
                        act.wait_ge(abs_done, 8 * n + k)
                    nc.scalar.activation(below[:, 0:D], raw[:].rearrange("p a b -> p (a b)")[:, k * D:(k + 1) * D],
                                         ACT.Abs, accum_out=abs_sum[:, n, k:k + 1]).then_inc(abs_done, 1)

            act.wait_ge(setup_act, 3)
            nc.scalar.activation(warm[:], minus1[:], ACT.Exp)
            norm_src(0, 0)
            split(0, xTp, xh_done, xT)
            v_tile(0, 0)
            v_tile(0, 1)
            act.wait_ge(xTp, 2)
            src_landed(act, 1, 1)
            normalise(LN_SRC, 1, src_sb[:, 1], xhat, (0, 1))
            k_exp(0, 0)
            v_tile(0, 2)
            v_tile(0, 3)
            k_exp(0, 1)
            act.wait_ge(bq_done, 2 * C)
            q_part(0)
            normalise(LN_SRC, 1, src_sb[:, 1], xhat, (2, 3))
            split(1, xTp, xh_done, xT)
            act.wait_ge(s_f1, 16)
            abs_sums(0, f1_raw, 0)
            attention_step(1, 1)
            act.wait_ge(w1_scaled, C)
            nc.scalar.activation(w1s[0][:].rearrange("p a b -> p (a b)"), w_scaled[:], ACT.Copy).then_inc(w_hi, 1)
            attention_step(2, 0)
            act.wait_ge(s_w2, 16)
            nc.scalar.activation(w2s[0][:], w2_raw[:], ACT.Copy).then_inc(w_hi, 1)
            attention_step(3, 1)
            abs_sums(0, f1_raw, 1)
            attention_step(4, 0)
            act.wait_ge(s_f2, 16)
            abs_sums(1, f2_raw, 0)
            with act.Fori(FIRST, LAST, 2) as i:
                attention_step(i, 1)
                attention_step(i + 1, 0)
            abs_sums(1, f2_raw, 1)
            for i in range(LAST, S - 1):
                attention_step(i, i % 2)
            act.wait_ge(s_x, 16)
            normalise(LN_X, 0, x_in, x1)
            kv_part(S - 1)
            split(S - 2, yTp, yh_done, yT)
            q_part(S - 1)
            split(0, x1Tp, x1h_done, x1T)

            def gelu(j, m):
                if m >= 3:
                    act.wait_ge(hl_done, M * j + m - 2)
                elif exists(j, 1):
                    act.wait_ge(hl_done, M * j)
                act.wait_ge(h_mm, M * j + m + 1)
                nc.scalar.activation(g_sb[:, m % 3], pH[:, m % 4], ACT.Gelu, bias=b1c[:, m:m + 1]).then_inc(g_done, 1)

            def norm_out(i, tiles):
                if exists(i, 2):
                    act.wait_ge(s_out, 16 * (i - 1))
                normalise(LN_Z, i - 1, z_sb, o_sb, tiles)

            def norm_x(j):
                act.wait_ge(x1Tp, 2 * j)
                act.wait_ge(s_x, 16 * (j + 1))
                normalise(LN_X, j, x_in, x1)

            def mlp_step(i, front, ahead):
                if front:
                    for m in range(HEAD):
                        gelu(i + 1, m)
                        if m == 3 and exists(i, 1):
                            norm_out(i, (0, 1))
                        if m == 2 and not exists(i, 1):
                            normalise(LN_R, 0, r2, x2)
                split(i, x2Tp, x2h_done, x2T)
                if front:
                    for m in range(HEAD, M):
                        gelu(i + 1, m)
                    if exists(i, 1):
                        norm_out(i, (2, 3))
                for m in range(M):
                    act.wait_ge(u_mm, M * i + m + 1)
                    if exists(i, 1):
                        act.wait_ge(ul_done, M * i)
                    nc.scalar.activation(u_sb[:, m], pH[:, m % 4], ACT.Relu,
                                         bias=cols[:, COL_FB1 + m:COL_FB1 + m + 1]).then_inc(u_done, 1)
                if not front:
                    norm_out(i, range(T))
                if ahead:
                    norm_x(i + 2)
                    split(i + 2, x1Tp, x1h_done, x1T)
                if front:
                    act.wait_ge(x2Tp, 2 * (i + 1))
                    act.wait_ge(x2b_done, i + 1)
                    normalise(LN_R, i + 1, r2, x2)

            gelu(0, 0)
            gelu(0, 1)
            split(S - 1, yTp, yh_done, yT)
            for m in range(2, M):
                gelu(0, m)
            norm_x(1)
            split(1, x1Tp, x1h_done, x1T)
            mlp_step(0, True, True)
            with act.Fori(1, S - 2) as i:
                mlp_step(i, True, True)
            mlp_step(S - 2, True, False)
            mlp_step(S - 1, False, False)
            act.wait_ge(s_out, 16 * (S - 1))
            for h in range(2):
                t = 2 * h
                act.wait_ge(last_scaled, 2 * h + 2)
                nc.scalar.activation(o_sb[:, t], z_sb[:, t], ACT.Identity, bias=nmr[LN_Z][:, t:t + 1],
                                     scale=rstd[LN_Z][:, t:t + 1]).then_inc(last_even, 1)

        @block.vector
        def _(dve):
            def stats(n, j, source, tiles=range(T)):
                for t in tiles:
                    nc.vector.bn_stats(bn[n][:, t], source[:, t]).then_inc(stats_done[n], 1)

            def src_stats(j, slot):
                src_landed(dve, j, slot)
                stats(LN_SRC, j, src_sb[:, slot])

            def aggregate(n, j):
                for level in range(4):
                    moments_level(level, dve, n, j)

            def split(j, hi_done, done, parts):
                for c in range(C):
                    dve.wait_ge(hi_done, 2 * j + c + 1)
                    nc.vector.tensor_tensor(parts[1][:, c], pT[:, c], parts[0][:, c].bitcast(F32),
                                            ALU.subtract).then_inc(done, 1)

            def residual(i, slot):
                for h in range(2):
                    dve.wait_ge(o_mm, 2 * i + h + 1)
                    if h == 0:
                        dve.wait_ge(srcb_done, i + 1)
                        if exists(i, 1):
                            dve.wait_ge(s_stored, 16 * i)
                    p = (pS if h == 0 else pA) if isinstance(i, int) and i == S - 1 else pA if h == 0 else pKV[:, 0]
                    nc.vector.tensor_tensor(x_sb[:, 2 * h:2 * h + 2], p.rearrange("p (t d) -> p t d", t=2),
                                            srcb[:, slot, 2 * h:2 * h + 2], ALU.add).then_inc(x_done, 1)

            def k_tile(i, t):
                dve.wait_ge(v_done, T * i + t + 1)
                nc.vector.tensor_tensor(k1[:, t], pKV[:, 1 - t % 2, 0:D], row_k1[:], ALU.add).then_inc(k1_done, 1)

            def k_features(i, h):
                dve.wait_ge(ek_done, 2 * i + h + 1)
                nc.vector.scalar_tensor_tensor(
                    out=kf[:, 2 * h:2 * h + 2], in0=ek[:, 2 * h:2 * h + 2], scalar=1.0,
                    in1=k1[:, 2 * h:2 * h + 2], op0=ALU.min, op1=ALU.max).then_inc(kf_done, 1)

            def q_features(i, m):
                dve.wait_ge(eq_done, 2 * i + m + 1)
                nc.vector.scalar_tensor_tensor(
                    out=qf[:, m], in0=pQ[:, m], scalar=bq_one[:, m:m + 1], in1=eq[:, m],
                    op0=ALU.add, op1=ALU.max).then_inc(qf_done, 1)

            def kv_state(i):
                st = pS[:, 0:C * VW].rearrange("p (c n) -> p c n", c=C)
                dve.wait_ge(s_mm, i + 1)
                nc.vector.tensor_tensor(kvm[:], st[:, :, 0:P],
                                        mask[:, 0:P].rearrange("p (o n) -> p o n", o=1).broadcast_to([P, C, P]),
                                        ALU.mult).then_inc(kvm_done, 1)
                for c in range(C):
                    nc.vector.tensor_scalar(kvz[:, c, P:KW], mask[:, P:KW], st[:, c, P:P + 1], None,
                                            ALU.mult).then_inc(kvz_done, 1)
                dve.wait_ge(kvm_done, i + 1)
                for c in range(C):
                    nc.vector.scalar_tensor_tensor(
                        out=kvz[:, c, 0:P], in0=bv_mask[:, c], scalar=st[:, c, P:P + 1], in1=kvm[:, c],
                        op0=ALU.mult, op1=ALU.add).then_inc(kvz_done, 1)

            def numerators(h):
                return (pQ[:] if h == 0 else pT[:]).rearrange("p t (c n) -> p (t c) n", c=C)

            def denominators(i, h):
                num = numerators(h)
                dve.wait_ge(num_mm, 2 * i + h + 1)
                nc.vector.tensor_scalar(den[:, h], num[:, :, P:KW], ATTN_EPS, None, ALU.max).then_inc(den_done, 1)
                dve.wait_ge(den_done, 2 * i + h + 1)
                nc.vector.reciprocal(rden[:, h], den[:, h]).then_inc(rden_done, 1)

            def divide(i, h):
                num = numerators(h)
                dve.wait_ge(rden_done, 2 * i + h + 1)
                nc.vector.tensor_tensor(
                    y_sb[:, 2 * h:2 * h + 2].rearrange("p t (c h e) -> p (t c) h e", c=C, h=HC),
                    num[:, :, 0:P].rearrange("p a (h e) -> p a h e", h=HC),
                    rden[:, h].rearrange("p a (h o) -> p a h o", o=1).broadcast_to([P, 2 * C, HC, HD]),
                    ALU.mult).then_inc(y_done, 1)

            def attention_step(i, slot, spare1=None, spare2=None, spare3=None):
                last = isinstance(i, int) and i == S - 1
                ahead = not last
                n, j = (LN_X, 0) if isinstance(i, int) and i == S - 2 else (LN_SRC, i + 2)
                k_tile(i, 0)
                if exists(i, 1):
                    divide(i - 1, 1)
                k_tile(i, 1)
                if spare1:
                    spare1()
                k_tile(i, 2)
                k_features(i, 0)
                k_tile(i, 3)
                if spare2:
                    spare2()
                k_features(i, 1)
                if exists(i, 1):
                    split(i - 1, yh_done, yl_done, yT)
                if ahead:
                    if n == LN_X:
                        dve.wait_ge(s_x, 16)
                        stats(LN_X, 0, x_in)
                    else:
                        src_stats(j, slot)
                    moments_level(0, dve, n, j)
                q_features(i, 0)
                if ahead:
                    moments_level(1, dve, n, j)
                q_features(i, 1)
                if ahead:
                    moments_level(2, dve, n, j)
                if spare3:
                    spare3()
                kv_state(i)
                if ahead:
                    moments_level(3, dve, n, j)
                    split(i + 1, xh_done, xl_done, xT)
                else:
                    split(0, x1h_done, x1l_done, x1T)
                if exists(i, 1):
                    residual(i - 1, 1 - slot)
                denominators(i, 0)
                divide(i, 0)
                denominators(i, 1)

            def ternary(k):
                n, quarter = k // 4, k % 4
                raw, q = ((f1_raw, fq1), (f2_raw, fq2))[n]
                part = slice(quarter * C * F // 4, (quarter + 1) * C * F // 4)
                raw, q = (x[:].rearrange("p a b -> p (a b)")[:, part] for x in (raw, q))
                nc.vector.tensor_scalar(below[:, part], raw, thr_neg[:, n:n + 1], None,
                                        ALU.is_lt).then_inc(below_done, 1)
                dve.wait_ge(below_done, k + 1)
                nc.vector.scalar_tensor_tensor(out=q, in0=raw, scalar=thr[:, n:n + 1], in1=below[:, part],
                                               op0=ALU.is_gt, op1=ALU.subtract).then_inc(tern_done, 1)

            def scale_w1(c):
                dve.wait_ge(s_w1, 16)
                dve.wait_ge(wsplit, 2 * C + 2)
                nc.vector.tensor_scalar(w_scaled[:, c * F:(c + 1) * F], w1_raw[:, c],
                                        cols[:, COL_G2 + c:COL_G2 + c + 1], None, ALU.mult).then_inc(w1_scaled, 1)

            def shift_b1():
                dve.wait_ge(b1_mm, 2)
                dve.wait_ge(s_mm, 2)
                nc.vector.tensor_tensor(b1c[:], pS[:, SIDE:SIDE + M], cols[:, COL_B1:COL_B1 + M],
                                        ALU.add).then_inc(b1c_done, 1)

            def abs_total():
                dve.wait_ge(abs_done, 16)
                nc.vector.tensor_reduce(abs_tot[:], abs_sum[:], AX.X, ALU.add).then_inc(thr_done, 1)

            def thresholds():
                dve.wait_ge(thr_mm, 1)
                dve.wait_ge(s_mm, LAST + 1)
                nc.vector.tensor_scalar(thr[:], pS[:, SIDE:SIDE + 2], 1.0 / (D * F), Q_EPS, ALU.mult,
                                        ALU.add).then_inc(thr_done, 1)
                dve.wait_ge(thr_done, 2)
                nc.vector.tensor_scalar(thr_neg[:], thr[:], -0.5, None, ALU.mult).then_inc(thr_done, 1)
                dve.wait_ge(thr_done, 3)
                nc.vector.tensor_scalar(thr[:], thr[:], 0.5, None, ALU.mult).then_inc(thr_done, 1)
                dve.wait_ge(thr_done, 4)

            dve.memset(ones[:], 1.0).then_inc(setup_dve, 1)
            src_stats(0, 0)
            aggregate(LN_SRC, 0)
            dve.wait_ge(s_vec, 16)
            dve.wait_ge(setup_dve, 1)
            for c in range(C):
                nc.vector.tensor_scalar(be1_wide[:, c], ones[:], cols[:, COL_BE1 + c:COL_BE1 + c + 1], None,
                                        ALU.mult).then_inc(setup_dve, 1)
            dve.wait_ge(s_wqkv, 16)
            qkv_g = w_scaled[:, 0:C * 3 * D].rearrange("p (c n) -> p c n", c=C)
            for c in range(C):
                nc.vector.tensor_scalar(qkv_g[:, c], qkv_raw[:, c], cols[:, COL_G1 + c:COL_G1 + c + 1], None,
                                        ALU.mult).then_inc(scaled, 1)
            dve.wait_ge(scaled, C)
            for c in range(C):
                nc.vector.tensor_copy(wqkv[0][:, c], qkv_g[:, c]).then_inc(wsplit, 1)
            for c in range(C):
                dve.wait_ge(wsplit, c + 1)
                nc.vector.tensor_tensor(wqkv[1][:, c], qkv_g[:, c], wqkv[0][:, c].bitcast(F32),
                                        ALU.subtract).then_inc(wsplit, 1)
            src_stats(1, 1)
            split(0, xh_done, xl_done, xT)
            aggregate(LN_SRC, 1)
            dve.wait_ge(setup_pe_mm, 2)
            dve.wait_ge(s_rows_kv, 16)
            nc.vector.scalar_tensor_tensor(out=row_k1[:], in0=pA[:, 0:D], scalar=1.0, in1=rows_kv[:, 0:D],
                                           op0=ALU.add, op1=ALU.add).then_inc(brow_done, 1)
            dve.wait_ge(s_wout, 16)
            nc.vector.tensor_copy(wout[0][:], out_raw[:]).then_inc(wsplit, 1)
            dve.wait_ge(wsplit, 2 * C + 1)
            nc.vector.tensor_tensor(wout[1][:], out_raw[:], wout[0][:].bitcast(F32),
                                    ALU.subtract).then_inc(wsplit, 1)
            dve.wait_ge(brow_done, 1)

            def more_biases():
                nc.vector.tensor_tensor(row_v[:], pA[:, D:2 * D], rows_kv[:, D:2 * D], ALU.add).then_inc(brow_done, 1)
                for m in range(C):
                    b = cols[:, COL_BQ + m:COL_BQ + m + 1]
                    nc.vector.tensor_scalar(bq_neg[:, m:m + 1], pS[:, m:m + 1], b, -1.0, ALU.add,
                                            ALU.mult).then_inc(bq_done, 1)
                    nc.vector.tensor_scalar(bq_one[:, m:m + 1], pS[:, m:m + 1], b, 1.0, ALU.add,
                                            ALU.add).then_inc(bq_done, 1)

            def v_bias():
                dve.wait_ge(bq_done, 2 * C)
                dve.wait_ge(s_mask, 16)
                dve.wait_ge(brow_done, 2)
                nc.vector.tensor_tensor(bv_mask[:], row_v[:].rearrange("p (c n) -> p c n", c=C),
                                        mask[:, 0:P].rearrange("p (o n) -> p o n", o=1).broadcast_to([P, C, P]),
                                        ALU.mult).then_inc(brow_done, 1)
                dve.wait_ge(brow_done, 3)

            attention_step(0, 0, more_biases, v_bias)
            attention_step(1, 1, lambda: scale_w1(0), lambda: scale_w1(1), shift_b1)
            for i in range(2, FIRST):
                attention_step(i, i % 2)
            with dve.Fori(FIRST, LAST, 2) as i:
                attention_step(i, 1)
                attention_step(i + 1, 0)
            attention_step(LAST, 1, None, abs_total, thresholds)
            for n in range(4):
                attention_step(LAST + 1 + n, (LAST + 1 + n) % 2, lambda: ternary(2 * n), lambda: ternary(2 * n + 1))

            def split_gelu(j, m):
                dve.wait_ge(g_done, M * j + m + 1)
                nc.vector.tensor_copy(hT[0][:, m], g_sb[:, m % 3]).then_inc(hh_done, 1)
                dve.wait_ge(hh_done, M * j + m + 1)
                nc.vector.tensor_tensor(hT[1][:, m], g_sb[:, m % 3], hT[0][:, m].bitcast(F32),
                                        ALU.subtract).then_inc(hl_done, 1)

            def x_stats(j):
                dve.wait_ge(s_x, 16 * (j + 1))
                stats(LN_X, j, x_in)
                aggregate(LN_X, j)

            def mlp_output(j, ahead):
                for h in range(2):
                    if h == 0:
                        dve.wait_ge(r_done, 2 * (j + 1))
                        if exists(j, 1):
                            dve.wait_ge(x2_done, T * j)
                    dve.wait_ge(w2_mm, 2 * j + h + 1)
                    nc.vector.tensor_tensor(r2[:, 2 * h:2 * h + 2], pO[:, h].rearrange("p (t d) -> p t d", t=2),
                                            r_sb[:, 2 * h:2 * h + 2], ALU.add).then_inc(r2_done, 1)
                    dve.wait_ge(r2_done, 2 * j + h + 1)
                    stats(LN_R, j, r2, (2 * h, 2 * h + 1))
                    if h == 0 and ahead:
                        split(j + 1, x1h_done, x1l_done, x1T)
                aggregate(LN_R, j)

            def mlp_step(i, front, ahead):
                if front:
                    for m in range(HEAD - 1):
                        split_gelu(i + 1, m)
                split(i, x2h_done, x2l_done, x2T)
                if front:
                    for m in range(HEAD - 1, M):
                        split_gelu(i + 1, m)
                else:
                    aggregate(LN_Z, i - 1)
                if ahead:
                    x_stats(i + 2)
                for m in range(M):
                    dve.wait_ge(u_done, M * i + m + 1)
                    nc.vector.tensor_copy(uT[0][:, m], u_sb[:, m]).then_inc(uh_done, 1)
                    if not front and m % 2:
                        dve.wait_ge(uh_done, M * i + m + 1)
                        nc.vector.tensor_tensor(uT[1][:, m], u_sb[:, m], uT[0][:, m].bitcast(F32),
                                                ALU.subtract).then_inc(ul_odd, 1)
                if front:
                    mlp_output(i + 1, ahead)
                for h in range(2):
                    if front:
                        ffn_output(i, h)
                    else:
                        last_output(2 * h)
                        last_output(2 * h + 1)
                        last_moments(h)
                if ahead:
                    aggregate(LN_Z, i)

            def ffn_output(i, h):
                if h == 0:
                    dve.wait_ge(x2b_done, i + 1)
                    if exists(i, 1):
                        dve.wait_ge(out_done, T * i)
                dve.wait_ge(f_mm, 2 * i + h + 1)
                nc.vector.tensor_tensor(z_sb[:, 2 * h:2 * h + 2], pO[:, h].rearrange("p (t d) -> p t d", t=2),
                                        x2b[:, 2 * h:2 * h + 2], ALU.add).then_inc(z_done, 1)
                dve.wait_ge(z_done, 2 * i + h + 1)
                stats(LN_Z, i, z_sb, (2 * h, 2 * h + 1))

            def last_output(t):
                if t == 0:
                    dve.wait_ge(x2b_done, S)
                    dve.wait_ge(out_done, T * (S - 1))
                dve.wait_ge(last_mm, t + 1)
                nc.vector.tensor_tensor(z_sb[:, t], last_bank(t), x2b[:, t], ALU.add).then_inc(last_z, 1)
                dve.wait_ge(last_z, t + 1)
                stats(LN_Z, S - 1, z_sb, (t,))

            def last_moments(h):
                pair, dif, var = (x[:, 2 * h:2 * h + 2] for x in moments[LN_Z])
                b = bn[LN_Z][:, 2 * h:2 * h + 2]
                dve.wait_ge(stats_done[LN_Z], T * (S - 1) + 2 * h + 2)
                nc.vector.tensor_tensor(pair, b[:, :, 1:3], b[:, :, 4:6], ALU.add).then_inc(last_levels, 1)
                nc.vector.tensor_tensor(dif, b[:, :, 1], b[:, :, 4], ALU.subtract).then_inc(last_levels, 1)
                dve.wait_ge(last_levels, 4 * h + 1)
                nc.vector.tensor_scalar(nmean[LN_Z][:, 2 * h:2 * h + 2], pair[:, :, 0], -0.5, None,
                                        ALU.mult).then_inc(last_moments_done, 1)
                dve.wait_ge(last_levels, 4 * h + 2)
                nc.vector.scalar_tensor_tensor(out=dif, in0=dif, scalar=0.25, in1=dif, op0=ALU.mult,
                                               op1=ALU.mult).then_inc(last_levels, 1)
                dve.wait_ge(last_levels, 4 * h + 3)
                nc.vector.scalar_tensor_tensor(out=var, in0=pair[:, :, 1], scalar=1.0 / D, in1=dif,
                                               op0=ALU.mult, op1=ALU.add).then_inc(last_levels, 1)
                dve.wait_ge(last_levels, 4 * h + 4)
                nc.vector.tensor_scalar(veps[LN_Z][:, 2 * h:2 * h + 2], var, LN_EPS, None,
                                        ALU.add).then_inc(last_moments_done, 1)

            divide(S - 1, 1)
            split_gelu(0, 0)
            split_gelu(0, 1)
            split(S - 1, yh_done, yl_done, yT)
            split_gelu(0, 2)
            for m in range(3, M):
                split_gelu(0, m)
            residual(S - 1, 1)
            x_stats(1)
            mlp_output(0, True)
            mlp_step(0, True, True)
            with dve.Fori(1, S - 2) as i:
                mlp_step(i, True, True)
            mlp_step(S - 2, True, False)
            mlp_step(S - 1, False, False)
            dve.wait_ge(s_out, 16 * (S - 1))
            for h in range(2):
                t = 2 * h + 1
                dve.wait_ge(last_scaled, 2 * h + 2)
                nc.vector.tensor_scalar(o_sb[:, t], z_sb[:, t], rstd[LN_Z][:, t:t + 1], nmr[LN_Z][:, t:t + 1],
                                        ALU.mult, ALU.add).then_inc(last_odd, 1)

        @block.tensor
        def _(pe):
            def transposes(src_tile, ready):
                for c in range(C):
                    for t in range(T):
                        mm = nc.tensor.transpose(pT[:, c, t * P:(t + 1) * P], src_tile[:, t, c * P:(c + 1) * P],
                                                 ident[:])
                    mm.then_inc(ready, 1)

            def split_product(out_ap, lhs, rhs, chunks):
                for n, (a, w) in enumerate(passes3):
                    for c in range(chunks):
                        mm = nc.tensor.matmul(out_ap, lhs(a, w, c), rhs(a, w, c), start=n == 0 and c == 0,
                                              stop=n == 2 and c == chunks - 1)
                return mm

            def out_projection(i, pair0, pair1, ready):
                for t in range(T):
                    o = (pair0 if t < 2 else pair1)[:, t % 2 * D:(t % 2 + 1) * D]
                    mm = split_product(o, lambda a, w, c: yT[a][:, c, t * P:(t + 1) * P],
                                       lambda a, w, c: wout[w][:, c], C)
                    if t % 2:
                        mm.then_inc(ready, 1)

            def attention_step(i, before_state=None):
                pe.wait_ge(xh_done, 2 * i + 2)
                pe.wait_ge(xl_done, 2 * i + 2)
                for t in range(T):
                    if t == 1 and exists(i, 2):
                        pe.wait_ge(x_done, 2 * (i - 1))
                    if t >= 2:
                        pe.wait_ge(k1_done, T * i + t - 1)
                        pe.wait_ge(v_done, T * i + t - 1)
                    split_product(pKV[:, 1 - t % 2], lambda a, w, c: xT[a][:, c, t * P:(t + 1) * P],
                                  lambda a, w, c: wqkv[w][:, c, D:3 * D], C).then_inc(kv_mm, 1)
                if exists(i, 1):
                    pe.wait_ge(y_done, 2 * i)
                    transposes(y_sb, yTp)
                for m in range(C):
                    split_product(pQ[:, m], lambda a, w, c: wqkv[w][:, c, m * P:(m + 1) * P],
                                  lambda a, w, c: xT[a][:, c], C).then_inc(q_mm, 1)
                if before_state:
                    before_state()
                pe.wait_ge(kf_done, 2 * i + 2)
                pe.wait_ge(v_done, T * i + T)
                for c in range(C):
                    for t in range(T):
                        mm = nc.tensor.matmul(pS[:, c * VW:(c + 1) * VW], kf[:, t, c * P:(c + 1) * P],
                                              v_sb[:, t, c], start=t == 0, stop=t == T - 1)
                mm.then_inc(s_mm, 1)
                if exists(i, 1):
                    pe.wait_ge(yh_done, 2 * i)
                    pe.wait_ge(yl_done, 2 * i)
                if isinstance(i, int) and i == S - 1:
                    pe.wait_ge(x1_done, T)
                    transposes(x1, x1Tp)
                else:
                    pe.wait_ge(xhat_done, T * (i + 1) + T)
                    transposes(xhat, xTp)
                if exists(i, 1):
                    out_projection(i - 1, pA, pKV[:, 0], o_mm)
                pe.wait_ge(kvz_done, 2 * C * (i + 1))
                pe.wait_ge(qf_done, 2 * i + 2)
                for t in range(T):
                    if t == 2:
                        if isinstance(i, int) and i == S - 1:
                            pe.wait_ge(x1l_done, 2)
                        else:
                            pe.wait_ge(xl_done, 2 * (i + 2))
                    for c in range(C):
                        mm = nc.tensor.matmul((pQ if t < 2 else pT)[:, t % 2, c * D:c * D + KW],
                                              qf[:, c, t * P:(t + 1) * P], kvz[:, c], start=True, stop=True)
                    if t % 2:
                        mm.then_inc(num_mm, 1)

            pe.wait_ge(s_vec, 16)
            pe.wait_ge(s_wqkv, 16)
            for m in range(C):
                for c in range(C):
                    mm = nc.tensor.matmul(pS[:, m:m + 1], qkv_raw[:, c, m * P:(m + 1) * P],
                                          cols[:, COL_BE1 + c:COL_BE1 + c + 1], start=c == 0, stop=c == C - 1)
            mm.then_inc(setup_pe_mm, 1)
            pe.wait_ge(setup_dve, 1 + C)

            def shift_kv(c):
                return nc.tensor.matmul(pA, be1_wide[:, c], qkv_raw[:, c, D:3 * D], start=c == 0, stop=c == C - 1)

            shift_kv(0)
            pe.wait_ge(s_const, 16)
            pe.wait_ge(xhat_done, T)
            transposes(xhat, xTp)
            shift_kv(1).then_inc(setup_pe_mm, 1)
            pe.wait_ge(wsplit, 2 * C)

            def shift_w1(half):
                pe.wait_ge(bq_done, 2 * C)
                pe.wait_ge(s_w1, 16)
                for m in range(half * M // 2, (half + 1) * M // 2):
                    for c in range(C):
                        mm = nc.tensor.matmul(pS[:, SIDE + m:SIDE + m + 1], w1_raw[:, c, m * P:(m + 1) * P],
                                              cols[:, COL_BE2 + c:COL_BE2 + c + 1], start=c == 0, stop=c == C - 1)
                mm.then_inc(b1_mm, 1)

            def abs_over_partitions():
                pe.wait_ge(thr_done, 1)
                nc.tensor.matmul(pS[:, SIDE:SIDE + 2], ones[:], abs_tot[:], start=True, stop=True).then_inc(thr_mm, 1)

            attention_step(0, before_state=lambda: shift_w1(0))
            pe.wait_ge(wsplit, 2 * C + 2)
            attention_step(1, before_state=lambda: shift_w1(1))
            attention_step(2, before_state=lambda: pe.wait_ge(b1c_done, 1))
            for i in range(3, FIRST):
                attention_step(i)
            with pe.Fori(FIRST, LAST) as i:
                attention_step(i)
            attention_step(LAST, before_state=abs_over_partitions)
            attention_step(LAST + 1, before_state=lambda: pe.wait_ge(thr_done, 2))
            for i in range(LAST + 2, S):
                attention_step(i)

            def mlp_up(j, m):
                if m >= 4:
                    pe.wait_ge(g_done, M * j + m - 3)
                split_product(pH[:, m % 4], lambda a, w, c: w1s[w][:, c, m * P:(m + 1) * P],
                              lambda a, w, c: x1T[a][:, c], C).then_inc(h_mm, 1)

            def mlp_down(j, ahead):
                pe.wait_ge(hh_done, M * (j + 1))
                pe.wait_ge(hl_done, M * (j + 1))
                for t in range(T):
                    if t == (2 if exists(j, 1) else 3) and ahead:
                        pe.wait_ge(x1_done, T * (j + 2))
                        transposes(x1, x1Tp)
                    if t % 2 == 0 and exists(j, 2):
                        pe.wait_ge(z_done, 2 * (j - 2) + t // 2 + 1)
                    elif t % 2 == 0 and isinstance(j, int) and j == 0:
                        pe.wait_ge(x_done, 2 * (S - 1) + t // 2 + 1)
                    mm = split_product(pO[:, t // 2, t % 2 * D:(t % 2 + 1) * D],
                                       lambda a, w, m: hT[a][:, m, t * P:(t + 1) * P],
                                       lambda a, w, m: w2s[w][:, m], M)
                    if t % 2:
                        mm.then_inc(w2_mm, 1)

            def ffn_up(i, front):
                pe.wait_ge(x2h_done, 2 * (i + 1))
                if front:
                    pe.wait_ge(x2l_done, 2 * (i + 1))

                def part(m, a):
                    for c in range(C):
                        mm = nc.tensor.matmul(pH[:, m % 4], fq1[:, c, m * P:(m + 1) * P], x2T[a][:, c],
                                              start=a == 0 and c == 0, stop=a == 1 and c == C - 1)
                    return mm

                if not front:
                    for m in range(4):
                        part(m, 0)
                    pe.wait_ge(x2l_done, 2 * (i + 1))
                for m in range(M):
                    if m < 4 and front:
                        pe.wait_ge(g_done, M * (i + 1) + m + 5)
                    if m >= 4:
                        pe.wait_ge(u_done, M * i + m - 3)
                    if m >= 4 or front:
                        part(m, 0)
                    part(m, 1).then_inc(u_mm, 1)

            def product(bank, t, a, m):
                return nc.tensor.matmul(bank, uT[a][:, m, t * P:(t + 1) * P], fq2[:, m],
                                        start=a == 0 and m == 0, stop=a == 1 and m == M - 1)

            def ffn_down(i):
                pe.wait_ge(uh_done, M * (i + 1))
                pe.wait_ge(ul_done, M * (i + 1))
                for t in range(T):
                    if t % 2 == 0:
                        pe.wait_ge(r2_done, 2 * (i + 1) + t // 2 + 1)
                    for a in range(2):
                        for m in range(M):
                            mm = product(pO[:, t // 2, t % 2 * D:(t % 2 + 1) * D], t, a, m)
                    if t % 2:
                        mm.then_inc(f_mm, 1)

            def last_ffn_down():
                pe.wait_ge(z_done, 2 * (S - 1))
                for m in range(M):
                    pe.wait_ge(uh_done, M * (S - 1) + m + 1)
                    for t in (0, 1):
                        product(last_bank(t), t, 0, m)
                for t in range(T):
                    for a in range(0 if t > 1 else 1, 2):
                        for m in range(M):
                            if t == 0:
                                pe.wait_ge(*last_low(m))
                            mm = product(last_bank(t), t, a, m)
                    mm.then_inc(last_mm, 1)

            def mlp_step(i, front, ahead):
                if front:
                    pe.wait_ge(x1h_done, 2 * (i + 2))
                    pe.wait_ge(x1l_done, 2 * (i + 2))
                    for m in range(HEAD):
                        mlp_up(i + 1, m)
                pe.wait_ge(x2_done, T * (i + 1))
                transposes(x2, x2Tp)
                if front:
                    for m in range(HEAD, M):
                        mlp_up(i + 1, m)
                ffn_up(i, front)
                if front:
                    mlp_down(i + 1, ahead)
                    ffn_down(i)
                else:
                    last_ffn_down()

            pe.wait_ge(x1h_done, 2)
            pe.wait_ge(x1l_done, 2)
            pe.wait_ge(b1c_done, 1)
            pe.wait_ge(tern_done, 8)
            pe.wait_ge(w_lo, 2)
            pe.wait_ge(x_done, 2 * (S - 1))
            pe.wait_ge(k1_done, T * S)
            mlp_up(0, 0)
            mlp_up(0, 1)
            pe.wait_ge(y_done, 2 * S)
            transposes(y_sb, yTp)
            for m in range(2, M):
                mlp_up(0, m)
            pe.wait_ge(yh_done, 2 * S)
            pe.wait_ge(yl_done, 2 * S)
            out_projection(S - 1, pS, pA, o_mm)
            mlp_down(0, True)
            mlp_step(0, True, True)
            with pe.Fori(1, S - 2) as i:
                mlp_step(i, True, True)
            mlp_step(S - 2, True, False)
            mlp_step(S - 1, False, False)


def kernel(L0_attn_src, L0_attn_qkv_w, L0_attn_qkv_b, L0_attn_out_w, L0_attn_out_b, L0_attn_w1, L0_attn_b1,
           L0_attn_w2, L0_attn_b2, L0_attn_g1, L0_attn_be1, L0_attn_g2, L0_attn_be2, L0_ffn_W1, L0_ffn_b1,
           L0_ffn_W2, L0_ffn_b2):
    import numpy as np
    import concourse.bacc as bacc
    from concourse.bass_utils import run_bass_kernel_spmd

    def column(v):
        return np.asarray(v).reshape(-1, P).T

    qkv_b = np.asarray(L0_attn_qkv_b)
    cols = np.concatenate([column(v) for v in (L0_attn_g1, L0_attn_be1, L0_attn_g2, L0_attn_be2, qkv_b[:D],
                                               L0_attn_b1, L0_ffn_b1)], axis=1)
    rows = np.concatenate([qkv_b[D:], np.asarray(L0_attn_out_b), np.asarray(L0_attn_b2), np.asarray(L0_ffn_b2)])
    head = np.arange(P) // HD
    const = np.concatenate([np.eye(P), head[:, None] == head[None, :], head[:, None] == np.arange(HC)[None, :]],
                           axis=1).astype(np.float32)
    arrays = {
        "src": L0_attn_src, "qkv_w": L0_attn_qkv_w, "out_w": L0_attn_out_w, "w1": L0_attn_w1, "w2": L0_attn_w2,
        "fw1": np.asarray(L0_ffn_W1).T, "fw2": np.asarray(L0_ffn_W2).T, "cols": cols, "rows": rows[None, :],
        "const": const,
    }
    arrays = {name: np.ascontiguousarray(a) for name, a in arrays.items()}
    nc = bacc.Bacc("TRN2", target_bir_lowering=False, num_devices=1)
    args = [nc.dram_tensor(name + "_dram", a.shape, mybir.dt.from_np(a.dtype), kind="ExternalInput").ap()
            for name, a in arrays.items()]
    out = nc.dram_tensor("out_dram", (S, N, D), F32, kind="ExternalOutput").ap()
    build(nc, *args, out)
    r = run_bass_kernel_spmd(nc, [{name + "_dram": a for name, a in arrays.items()}], core_ids=[0])
    return r.results[0]["out_dram"]
```
